# Optimizing a Trainium2 kernel written in Bass

```python
import numpy as np
import jax
import jax.numpy as jnp

def _softmax(x, axis=-1):
    return jax.nn.softmax(x, axis=axis)

def _gelu(x):
    return jax.nn.gelu(x, approximate=True)

def _silu(x):
    return jax.nn.silu(x)

def _sigmoid(x):
    return jax.nn.sigmoid(x)

def _layernorm(x, axis=-1, eps=1e-05):
    m = jnp.mean(x, axis=axis, keepdims=True)
    v = jnp.var(x, axis=axis, keepdims=True)
    return (x - m) / jnp.sqrt(v + eps)

def _scatter_add(tgt, idx, src, axis=0):
    return tgt.at[idx].add(src)

def _segment_sum(src, seg, n):
    return jax.ops.segment_sum(src, seg, n)
kernel_name = 'mk_adj_preln_d2_adj_r2_a67a7a'

def setup_inputs(seed: int=0):
    np.random.seed(seed)
    _w = jnp.asarray

    def _rec_inputs():
        import jax
        import jax.numpy as jnp
        _gk = jax.random.key(seed)
        x = -0.0005207 + 1.001 * jax.random.normal(jax.random.fold_in(_gk, 1), (4096, 128), jnp.float32)
        _a = jax.random.bernoulli(jax.random.fold_in(_gk, 2), 0.00390625, (4096, 4096))
        adj = _a.astype(jnp.int32)
        return (x, adj)
    x, adj = _rec_inputs()

    def _L0_gnn_setup():
        import jax, jax.numpy as jnp
        import numpy as np
        NEG_INF = -9000000000000000.0
        key = jax.random.key(seed)
        k1, k2, k3, k4 = jax.random.split(key, 4)
        N, F_IN, F_OUT = (4096, 128, 128)
        x = jax.random.normal(k1, (N, F_IN), dtype=jnp.float32)
        adj = jax.random.randint(k2, (N, N), 0, 2, dtype=jnp.int32)
        W = jax.random.normal(k3, (F_OUT, F_IN), dtype=jnp.float32) * (1.0 / np.sqrt(F_IN))
        a = jax.random.normal(k4, (2 * F_OUT,), dtype=jnp.float32) * (1.0 / np.sqrt(2 * F_OUT))
        return {'x': x, 'adj': adj, 'W': W, 'a': a}
    _L0_gnn_all = _L0_gnn_setup()
    _L0_gnn_in = {k: v for k, v in _L0_gnn_all.items() if k in ('W', 'a')}
    del _L0_gnn_all

    def _L1_gnn_setup():
        import jax, jax.numpy as jnp
        import numpy as np
        N = 4096
        IN_FEATS = 128
        OUT_FEATS = 128
        key = jax.random.key(seed)
        k_adj, k_x, k_att, k_w = jax.random.split(key, 4)
        adjacency = jax.random.randint(k_adj, (N, N), 0, 2, dtype=jnp.int32)
        inputs = jax.random.normal(k_x, (N, IN_FEATS), dtype=jnp.float32)
        attention_projection = jax.random.normal(k_att, (N, N), dtype=jnp.float32)
        W = jax.random.normal(k_w, (IN_FEATS, OUT_FEATS), dtype=jnp.float32) / np.sqrt(IN_FEATS)
        b = jnp.zeros((OUT_FEATS,), dtype=jnp.float32)
        return {'adjacency': adjacency, 'inputs': inputs, 'attention_projection': attention_projection, 'W': W, 'b': b}
    _L1_gnn_all = _L1_gnn_setup()
    _L1_gnn_in = {k: v for k, v in _L1_gnn_all.items() if k in ('W', 'b')}
    del _L1_gnn_all
    return {'x': x, 'adj': adj, 'L0_gnn_W': _L0_gnn_in['W'], 'L0_gnn_a': _L0_gnn_in['a'], 'L1_gnn_W': _L1_gnn_in['W'], 'L1_gnn_b': _L1_gnn_in['b']}

def reference(x, adj, L0_gnn_W, L0_gnn_a, L1_gnn_W, L1_gnn_b):
    import jax
    import jax.numpy as jnp

    def _L0_gnn_ref(x, adj, W, a):
        import jax, jax.numpy as jnp
        import numpy as np
        NEG_INF = -9000000000000000.0
        h = x @ W.T
        F_OUT = h.shape[1]
        a1, a2 = (a[:F_OUT], a[F_OUT:])
        s_i = h @ a1
        s_j = h @ a2
        e = jax.nn.leaky_relu(s_i[:, None] + s_j[None, :], negative_slope=0.2)
        att = jnp.where(adj > 0, e, jnp.asarray(NEG_INF, dtype=e.dtype))
        att = jax.nn.softmax(att, axis=1)
        h_prime = att @ h
        return h_prime

    def _L1_gnn_ref(adjacency, inputs, attention_projection, W, b):
        import jax, jax.numpy as jnp
        import numpy as np
        N = 4096
        IN_FEATS = 128
        OUT_FEATS = 128
        adj = adjacency.astype(attention_projection.dtype)
        x = attention_projection * adj @ inputs
        x = jax.nn.relu(x @ W + b)
        return x
    h = jnp.maximum(_layernorm(x, axis=-1), 0.0)
    x = x + _L0_gnn_ref(h, adj, L0_gnn_W, L0_gnn_a)
    h = jnp.maximum(_layernorm(x, axis=-1), 0.0)
    x = x + _L1_gnn_ref(adj, h, adj, L1_gnn_W, L1_gnn_b)
    return x

_drawn_inputs = setup_inputs


def setup_inputs(seed=0):
    import zlib

    import numpy as np

    out = dict(_drawn_inputs(seed))
    spreads = {'L1_gnn_b': (0.0, 0.553)}
    factors = {}
    for name, (base, spread) in spreads.items():
        noise = np.random.default_rng([zlib.crc32(name.encode()), seed]).standard_normal(out[name].shape)
        drawn = base * np.exp(spread * noise) if base else spread * noise
        out[name] = jnp.asarray(drawn.astype(out[name].dtype))
    for name, factor in factors.items():
        out[name] = (out[name] * factor).astype(out[name].dtype)
    return out
```

```python
from contextlib import ExitStack

import concourse.bass as bass
from concourse import mybir

ALU = mybir.AluOpType
ACT = mybir.ActivationFunctionType
F32 = mybir.dt.float32
F16 = mybir.dt.float16
F8 = mybir.dt.float8e4
U8 = mybir.dt.uint8
U32 = mybir.dt.uint32
I32 = mybir.dt.int32
AX_X = mybir.AxisListType.X

P = 128
N = 4096
F = 128
NJ = N // P
IG = 512
NG = N // IG
NB = IG // P
CJ = 4
NCH = NJ // CJ
HJ = 2
RAW = 4
CH = CJ * IG
SLOTS = 5
SPILL = NG - SLOTS
ONE = 0x38
SC = 4096.0
EPS = 1e-5
W = F + 1
XQ = 4
QB = NJ // XQ


def ds(start, size):
    return bass.ds(start, size)


def wait_next(eng, sem, level, step):
    eng.wait_ge(sem, level)
    eng.reg_add(level, level, step)


def gat_sum_kernel(nc, x_in, adj_in, w0_in, w0t_in, a_in, w1_in, b1_in, out, spill):
    with ExitStack() as ctx:
        def sb(name, shape, dt):
            return ctx.enter_context(nc.sbuf_tensor(name, shape, dt))

        def ps(name):
            return ctx.enter_context(nc.psum_tensor(name, [P, 512], F32))

        def sem(name):
            return ctx.enter_context(nc.semaphore(name))

        M = sb("M", [P, SLOTS * NJ * IG], U8)
        raw = sb("raw", [P, RAW * HJ * IG], I32)
        key = sb("key", [P, 2 * CH], U8)
        pos = sb("pos", [P, 2 * CH], U8)
        neg = sb("neg", [P, 2 * CH], U8)
        s_row = sb("s_row", [P, N], F32)
        XAB = sb("XAB", [P, 2 * NJ * 2 * W], F16)
        XA = XAB[:, 0:NJ * 2 * W].rearrange("p (j k w) -> p j k w", k=2, w=W)
        XB = XAB[:, NJ * 2 * W:].rearrange("p (j k w) -> p j k w", k=2, w=W)
        h2 = sb("h2", [P, NJ * 2 * F], F16)
        x = sb("x", [P, NJ * F], F32)
        ident = sb("ident", [P, P], F32)
        ones = sb("ones", [P, P], F32)
        w0 = sb("w0", [P, F], F32)
        w0t = sb("w0t", [P, F], F32)
        w1 = sb("w1", [P, F], F32)
        b1 = sb("b1", [P, F], F32)
        a2 = sb("a2", [P, 2], F32)
        wa = sb("wa", [P, 2], F32)
        wrow = sb("wrow", [P, P], F32)
        st = sb("st", [P, NJ * 6], F32)
        mv = sb("mv", [P, NJ * 2], F32)
        sd = sb("sd", [P, NJ], F32)
        rs = sb("rs", [P, NJ], F32)
        s_cols = sb("s_cols", [P, NJ, 2], F32)
        nsj = sb("nsj", [P, NJ], F32)
        smx = sb("smx", [P, 1], F32)
        s1 = sb("s1", [1, 1], F32)
        S = sb("S", [P, 4], F32)
        et = sb("et", [P, 3 * NJ], F32)
        Fs = sb("Fs", [P, 2 * NJ], F32)
        Es = sb("Es", [P, 2 * NJ], F32)
        hsum = sb("hsum", [P, NG], F32)
        hcol = sb("hcol", [P, 1], F32)
        hrow = sb("hrow", [P, P], F32)
        lone = sb("lone", [P, W], F32)
        u = sb("u", [P, NB * W], F32)
        uT = sb("uT", [P, IG], F32)
        z = sb("z", [P, NB], F32)
        rv = sb("rv", [P, NB], F32)
        gst = sb("gst", [P, NB * 6], F32)
        gmv = sb("gmv", [P, NB * 2], F32)
        gsd = sb("gsd", [P, NB], F32)
        grs = sb("grs", [P, NB], F32)
        tt = sb("tt", [P, NB * F], F32)
        hnb = M[:, (SLOTS - 1) * NJ * IG:SLOTS * NJ * IG].bitcast(F32)
        hn = hnb
        hT = M[:, (SLOTS - 2) * NJ * IG:(SLOTS - 1) * NJ * IG].bitcast(F32)

        acc = [ps(f"acc{b}") for b in range(NB)]
        aux = [ps(f"aux{b}") for b in range(4)]

        x_here = [sem(f"x_here{q}") for q in range(XQ)]
        w_here = sem("w_here")
        raw_here = [sem(f"raw_here{b}") for b in range(RAW)]
        slot_free = sem("slot_free")
        mask_made = sem("mask_made")
        spilled = sem("spilled")
        back = sem("back")
        stored = sem("stored")
        ident_zero = sem("ident_zero")
        ident_made = sem("ident_made")
        dve_pro = sem("dve_pro")
        act_pro = sem("act_pro")
        pe_pro = sem("pe_pro")
        hn_made = sem("hn_made")
        row_made = sem("row_made")
        keys_made = sem("keys_made")
        pos_made = sem("pos_made")
        neg_made = sem("neg_made")
        block_summed = sem("block_summed")
        xab_made = sem("xab_made")
        u_high = sem("u_high")
        u_low = sem("u_low")
        u_made = sem("u_made")
        dve_epi = sem("dve_epi")
        u_whole = sem("u_whole")
        u_turned = sem("u_turned")
        ut_here = sem("ut_here")
        att_made = sem("att_made")
        x1_made = sem("x1_made")
        var_made = sem("var_made")
        sd_made = sem("sd_made")
        h2_made = sem("h2_made")
        agg_summed = sem("agg_summed")
        agg_here = sem("agg_here")
        y_made = sem("y_made")
        y_used = sem("y_used")
        o_made = sem("o_made")

        var_pro = sem("var_pro")
        rs_made = sem("rs_made")
        y_pro = sem("y_pro")
        wa_summed = sem("wa_summed")
        cols_summed = sem("cols_summed")
        smax_turned = sem("smax_turned")
        smax_spread = sem("smax_spread")
        row_summed = sem("row_summed")
        f_made = sem("f_made")
        xab_high = sem("xab_high")
        lone_made = sem("lone_made")
        lone_summed = sem("lone_summed")
        PRO_EXP = XQ + 12
        EPI = 10
        freed = sb("freed", [P, 1 + SPILL], F32)
        eps = sb("eps", [P, 1], F32)
        mv3 = mv[:, :].rearrange("p (j k) -> p j k", k=2)
        gmv3 = gmv[:, :].rearrange("p (j k) -> p j k", k=2)

        def back_of(g):
            w = NJ * IG
            if g < 2:
                return XAB[:, :].bitcast(U8)[:, g * w:(g + 1) * w]
            return s_row[:, :].bitcast(U8)

        block = ctx.enter_context(nc.Block())

        @block.sync
        def _(sp):
            for q in range(XQ):
                w = QB * F
                sp.dma_start(x[:, q * w:(q + 1) * w], x_in[:, q * w:(q + 1) * w]).then_inc(x_here[q], 16)
            sp.dma_start(w0[:, :], w0_in).then_inc(w_here, 16)
            sp.dma_start(a2[:, :], a_in).then_inc(w_here, 16)

            def load(g, h):
                b = h % RAW
                sp.dma_start(raw[:, b * HJ * IG:(b + 1) * HJ * IG],
                             adj_in[ds(g * P, P), h * HJ * IG:(h + 1) * HJ * IG]).then_inc(raw_here[b], 16)

            for h in range(RAW):
                load(0, h)
            sp.dma_start(w0t[:, :], w0t_in).then_inc(w_here, 16)
            sp.dma_start(w1[:, :], w1_in).then_inc(w_here, 16)
            sp.dma_start(b1[:, :], b1_in.partition_broadcast(P)).then_inc(w_here, 16)
            for h in range(RAW, 2 * NCH):
                sp.wait_ge(mask_made, h - RAW + 1)
                load(0, h)
            with sp.Fori(1, NG) as g:
                for h in range(2 * NCH):
                    sp.wait_ge(mask_made, g * 2 * NCH + (h - RAW + 1))
                    load(g, h)
            for g in range(NG):
                sp.wait_ge(o_made, (g + 1) * NB)
                w = IG
                i = (g + SPILL) % NG
                sp.dma_start(out[:, i * w:(i + 1) * w], x[:, i * w:(i + 1) * w]).then_inc(stored, 16)
            sp.wait_ge(stored, 16 * NG)

        @block.gpsimd
        def _(pool):
            nc.gpsimd.memset(ident[:, :], 0.0).then_inc(ident_zero, 1)
            nc.gpsimd.memset(ones[:, :], 1.0).then_inc(ident_zero, 1)
            pool.wait_ge(ident_zero, 2)
            nc.gpsimd.affine_select(out=ident[:, :], in_=ident[:, :], compare_op=ALU.not_equal, fill=1.0,
                                    base=0, pattern=[[-1, P]], channel_multiplier=1).then_inc(ident_made, 1)
            nc.gpsimd.memset(freed[:, 0:1], 0.0).then_inc(slot_free, SLOTS)
            for g in range(SPILL):
                pool.wait_ge(mask_made, (g + 1) * 2 * NCH)
                pool.wait_ge(neg_made, (g + 1) * NCH)
                w = NJ * IG
                pool.dma_start(spill[:, g * w:(g + 1) * w], M[:, g * w:(g + 1) * w]).then_inc(spilled, 16)
                pool.wait_ge(spilled, 16 * (g + 1))
                nc.gpsimd.memset(freed[:, g + 1:g + 2], 0.0).then_inc(slot_free, 1)
            pool.wait_ge(block_summed, NG * NCH * NB)
            for g in range(SPILL):
                pool.dma_start(back_of(g), spill[:, g * w:(g + 1) * w]).then_inc(back, 16)

        @block.scalar
        def _(act):
            for q in range(XQ):
                act.wait_ge(dve_pro, q + 1)
                nc.scalar.activation(sd[:, q * QB:(q + 1) * QB],
                                     mv3[:, q * QB:(q + 1) * QB, 1],
                                     ACT.Sqrt, bias=eps[:, 0:1]).then_inc(act_pro, 1)
            for g in range(NG):
                act.wait_ge(pe_pro, g + 1)
                nc.scalar.activation(hT[:, g * IG:(g + 1) * IG], aux[g % 2][:, :], ACT.Copy,
                                     accum_out=hsum[:, g:g + 1]).then_inc(act_pro, 1)
            act.wait_ge(dve_pro, PRO_EXP)
            nc.scalar.activation(Fs[:, 0:NJ], et[:, 0:NJ], ACT.Exp).then_inc(act_pro, 1)
            nc.scalar.activation(Fs[:, NJ:], et[:, 0:NJ], ACT.Exp, scale=0.2).then_inc(act_pro, 1)
            nc.scalar.activation(Es[:, :], et[:, NJ:3 * NJ], ACT.Exp).then_inc(act_pro, 1)

            def masks(g, c):
                for k in range(2):
                    h = 2 * c + k
                    b = h % RAW
                    act.wait_ge(raw_here[b], 16 * (g * (2 * NCH // RAW) + h // RAW + 1))
                    nc.scalar.activation(M[:, ds((g % SLOTS) * (NJ * IG) + h * HJ * IG, HJ * IG)],
                                         raw[:, b * HJ * IG:(b + 1) * HJ * IG],
                                         ACT.Copy, scale=float(ONE)).then_inc(mask_made, 1)

            def high_parts(g):
                for b in range(NB):
                    act.wait_ge(block_summed, g * (NCH * NB) + ((NCH - 1) * NB + b + 1))
                    nc.scalar.activation(u[:, b * W:(b + 1) * W], acc[b][:, 0:W], ACT.Copy,
                                         scale=Es[:, ds(g * NB + b, 1)]).then_inc(u_high, 1)

            def turned(g):
                act.wait_ge(u_turned, g + 1)
                nc.scalar.activation(uT[:, :], aux[2][:, :], ACT.Copy).then_inc(ut_here, 1)

            def deviations(g):
                act.wait_ge(var_made, g + 1)
                nc.scalar.activation(gsd[:, :], gmv3[:, :, 1],
                                     ACT.Sqrt, bias=eps[:, 0:1]).then_inc(sd_made, 1)

            for c in range(NCH):
                masks(0, c)
            with act.Fori(1, NG) as g:
                act.wait_ge(slot_free, g + 1)
                for c in range(NCH):
                    masks(g, c)
                    if c == 1:
                        high_parts(g - 1)
                    if c == 3:
                        turned(g - 1)
                    if c == 5:
                        deviations(g - 1)
            high_parts(NG - 1)
            turned(NG - 1)
            deviations(NG - 1)
            for n in range(NG):
                act.wait_ge(agg_summed, n + 1)
                if n >= 1:
                    act.wait_ge(y_made, n)
                nc.scalar.activation(uT[:, :], acc[n % 2][:, :], ACT.Copy, scale=1.0 / SC).then_inc(agg_here, 1)

        @block.vector
        def _(dve):
            v = nc.vector
            x1_due = dve.alloc_register("x1_due")
            dve.reg_mov(x1_due, 1)
            stats_due = dve.alloc_register("stats_due")
            dve.reg_mov(stats_due, 3)
            n = [0]

            def step(ins):
                n[0] += 1
                ins.then_inc(dve_pro, 1)

            def settle():
                dve.wait_ge(dve_pro, n[0])

            v.memset(eps[:, :], EPS).then_inc(row_made, 1)
            v.memset(lone[:, F:W], float(N)).then_inc(row_made, 1)
            dve.wait_ge(row_made, 2)
            for q in range(XQ):
                dve.wait_ge(x_here[q], 16)
                for j in range(q * QB, (q + 1) * QB):
                    last = v.bn_stats(st[:, j * 6:(j + 1) * 6], x[:, j * F:(j + 1) * F])
                last.then_inc(var_pro, 1)
                dve.wait_ge(var_pro, q + 1)
                for j in range(q * QB, (q + 1) * QB):
                    last = v.bn_aggr(mv[:, 2 * j:2 * j + 2], st[:, j * 6:(j + 1) * 6])
                step(last)
            for q in range(XQ):
                r = slice(q * QB, (q + 1) * QB)
                dve.wait_ge(act_pro, q + 1)
                v.reciprocal(rs[:, r], sd[:, r]).then_inc(rs_made, 1)
                dve.wait_ge(rs_made, q + 1)
                for j in range(q * QB, (q + 1) * QB):
                    last = v.tensor_scalar(hn[:, j * F:(j + 1) * F], x[:, j * F:(j + 1) * F],
                                           mv[:, 2 * j:2 * j + 1], rs[:, j:j + 1], ALU.subtract, ALU.mult)
                last.then_inc(y_pro, 1)
                dve.wait_ge(y_pro, q + 1)
                w = QB * F
                v.tensor_scalar(hn[:, q * w:(q + 1) * w], hn[:, q * w:(q + 1) * w], 0.0, None,
                                ALU.max).then_inc(hn_made, 1)
            dve.wait_ge(wa_summed, 1)
            step(v.tensor_copy(wa[:, :], aux[3][:, 0:2]))
            settle()
            step(v.tensor_copy(wrow[:, :], wa[:, 0:1].to_broadcast([P, P])))
            dve.wait_ge(cols_summed, 1)
            step(v.tensor_copy(s_cols[:, :, :].rearrange("p j k -> p (j k)"), aux[3][:, 64:64 + 2 * NJ]))
            settle()
            step(v.tensor_scalar(nsj[:, :], s_cols[:, :, 1], -1.0, None, ALU.mult))
            step(v.reduce_max(smx[:, :], s_cols[:, :, 1], AX_X))
            settle()
            dve.wait_ge(smax_turned, 1)
            step(v.reduce_max(s1[:, :], aux[2][0:1, 0:P], AX_X))
            dve.wait_ge(smax_spread, 1)
            step(v.tensor_copy(S[:, 0:1], aux[2][:, P:P + 1]))
            settle()
            step(v.tensor_scalar(et[:, 0:NJ], s_cols[:, :, 1], S[:, 0:1], None, ALU.subtract))
            step(v.tensor_scalar(et[:, NJ:2 * NJ], s_cols[:, :, 0], S[:, 0:1], None, ALU.add))
            settle()
            step(v.scalar_tensor_tensor(tt[:, 0:NJ], et[:, NJ:2 * NJ], 0.2, et[:, NJ:2 * NJ], ALU.mult, ALU.max))
            settle()
            step(v.scalar_tensor_tensor(et[:, 2 * NJ:], et[:, NJ:2 * NJ], 0.2, tt[:, 0:NJ], ALU.mult, ALU.subtract))
            settle()
            step(v.tensor_tensor(et[:, NJ:2 * NJ], et[:, NJ:2 * NJ], tt[:, 0:NJ], ALU.subtract))
            settle()
            for g in range(NG):
                dve.wait_ge(row_summed, g + 1)
                v.tensor_copy(s_row[:, g * IG:(g + 1) * IG], acc[g % 2][:, :]).then_inc(row_made, 1)
            dve.wait_ge(row_made, 2 + NG)
            dve.wait_ge(act_pro, XQ + NG + 2)
            v.tensor_scalar(Fs[:, :], Fs[:, :], SC, None, ALU.mult).then_inc(f_made, 1)
            dve.wait_ge(f_made, 1)
            for k, X in enumerate((XA, XB)):
                fk = Fs[:, k * NJ:(k + 1) * NJ]
                v.tensor_copy(X[:, :, 0, F], fk).then_inc(f_made, 1)
                dve.wait_ge(f_made, 2 + 2 * k)
                v.tensor_tensor(X[:, :, 1, F], fk, X[:, :, 0, F], ALU.subtract).then_inc(f_made, 1)

            def parts(j):
                h = hn[:, j * F:(j + 1) * F]
                for k, X in enumerate((XA, XB)):
                    v.tensor_scalar(X[:, j, 0, 0:F], h, Fs[:, k * NJ + j:k * NJ + j + 1], None,
                                    ALU.mult).then_inc(xab_high, 1)
                dve.wait_ge(xab_high, 2 * (j + 1))
                for k, X in enumerate((XA, XB)):
                    last = v.scalar_tensor_tensor(X[:, j, 1, 0:F], h, Fs[:, k * NJ + j:k * NJ + j + 1],
                                                  X[:, j, 0, 0:F], ALU.mult, ALU.subtract)
                last.then_inc(xab_made, 1)

            def prepare(g, c, t):
                o = (c % 2) * CH
                for k in range(CJ):
                    j = c * CJ + k
                    last = v.tensor_scalar(key[:, o + k * IG:o + (k + 1) * IG], s_row[:, ds(g * IG, IG)],
                                           nsj[:, j:j + 1], float(ONE), ALU.is_gt, ALU.mult)
                last.then_inc(keys_made, 1)
                m = M[:, ds((g % SLOTS) * (NJ * IG) + c * CH, CH)].bitcast(U32)
                dve.wait_ge(mask_made, t * 2 + 2)
                if not (isinstance(t, int) and t < 2):
                    dve.wait_ge(block_summed, (t - 1) * NB)
                dve.wait_ge(keys_made, t + 1)
                v.tensor_tensor(pos[:, o:o + CH].bitcast(U32), m, key[:, o:o + CH].bitcast(U32),
                                ALU.bitwise_and).then_inc(pos_made, 1)
                dve.wait_ge(pos_made, t + 1)
                v.tensor_tensor(neg[:, o:o + CH].bitcast(U32), m, pos[:, o:o + CH].bitcast(U32),
                                ALU.bitwise_xor).then_inc(neg_made, 1)

            def lonely_sums():
                dve.wait_ge(act_pro, XQ + NG)
                v.reduce_sum(hcol[:, :], hsum[:, :], AX_X).then_inc(lone_made, 1)
                dve.wait_ge(lone_made, 1)
                v.tensor_copy(hrow[:, :], hcol[:, 0:1].to_broadcast([P, P])).then_inc(lone_made, 1)

            def gather(g):
                for b in range(NB):
                    dve.wait_ge(u_high, g * NB + b + 1)
                    ub = u[:, b * W:(b + 1) * W]
                    v.scalar_tensor_tensor(ub, acc[b][:, W:2 * W], Es[:, ds(g * NB + b, 1)], ub,
                                           ALU.mult, ALU.add).then_inc(u_low, 1)
                    dve.wait_ge(u_low, g * NB + b + 1)
                    v.scalar_tensor_tensor(ub, acc[b][:, 2 * W:3 * W], Es[:, ds(g * NB + (NJ + b), 1)], ub,
                                           ALU.mult, ALU.add).then_inc(u_made, 1)

            def complete(g):
                uw = u[:, :].rearrange("p (b w) -> p b w", w=W)
                dve.wait_ge(u_made, g * NB + NB)
                v.tensor_scalar(z[:, :], uw[:, :, F], 0.0, None, ALU.is_equal).then_inc(dve_epi, 1)
                dve.wait_ge(dve_epi, g * EPI + 1)
                for b in range(NB):
                    ub = u[:, b * W:(b + 1) * W]
                    last = v.scalar_tensor_tensor(ub, lone[:, :], z[:, b:b + 1], ub, ALU.mult, ALU.add)
                last.then_inc(u_whole, 1)
                dve.wait_ge(u_whole, g + 1)
                v.reciprocal(rv[:, :], uw[:, :, F]).then_inc(dve_epi, 1)

            def residual(g):
                dve.wait_ge(att_made, g + 1)
                dve.wait_ge(dve_epi, g * EPI + 2)
                for b in range(NB):
                    xb = x[:, ds(g * IG + b * F, F)]
                    last = v.scalar_tensor_tensor(xb, aux[3][:, b * F:(b + 1) * F], rv[:, b:b + 1], xb,
                                                  ALU.mult, ALU.add)
                last.then_inc(x1_made, 1)
                if isinstance(g, int):
                    dve.wait_ge(x1_made, g + 1)
                else:
                    wait_next(dve, x1_made, x1_due, 1)
                for b in range(NB):
                    last = v.bn_stats(gst[:, b * 6:(b + 1) * 6], x[:, ds(g * IG + b * F, F)])
                last.then_inc(dve_epi, 1)
                if isinstance(g, int):
                    dve.wait_ge(dve_epi, g * EPI + 3)
                else:
                    wait_next(dve, dve_epi, stats_due, EPI)
                for b in range(NB):
                    last = v.bn_aggr(gmv[:, 2 * b:2 * b + 2], gst[:, b * 6:(b + 1) * 6])
                last.then_inc(var_made, 1)

            def normal(g):
                dve.wait_ge(sd_made, g + 1)
                v.reciprocal(grs[:, :], gsd[:, :]).then_inc(dve_epi, 1)
                dve.wait_ge(dve_epi, g * EPI + 4)
                v.tensor_scalar(grs[:, :], grs[:, :], SC, None, ALU.mult).then_inc(dve_epi, 1)
                for b in range(NB):
                    v.tensor_scalar(tt[:, b * F:(b + 1) * F], x[:, ds(g * IG + b * F, F)],
                                    gmv[:, 2 * b:2 * b + 1], 0.0, ALU.subtract,
                                    ALU.max).then_inc(dve_epi, 1)
                dve.wait_ge(dve_epi, g * EPI + 9)
                for b in range(NB):
                    last = v.tensor_scalar(h2[:, ds(g * 2 * IG + 2 * b * F, F)], tt[:, b * F:(b + 1) * F],
                                           grs[:, b:b + 1], None, ALU.mult)
                last.then_inc(dve_epi, 1)
                dve.wait_ge(dve_epi, g * EPI + 10)
                for b in range(NB):
                    last = v.scalar_tensor_tensor(h2[:, ds(g * 2 * IG + (2 * b + 1) * F, F)],
                                                  tt[:, b * F:(b + 1) * F], grs[:, b:b + 1],
                                                  h2[:, ds(g * 2 * IG + 2 * b * F, F)],
                                                  ALU.mult, ALU.subtract)
                last.then_inc(h2_made, 1)

            for c in range(NCH):
                for k in range(CJ):
                    parts(c * CJ + k)
                prepare(0, c, c)
                if c == 1:
                    lonely_sums()
            dve.wait_ge(lone_summed, 1)
            v.tensor_copy(lone[:, 0:F], aux[0][:, 0:F]).then_inc(lone_made, 1)
            dve.wait_ge(lone_made, 3)
            with dve.Fori(1, NG) as g:
                for c in range(NCH):
                    prepare(g, c, g * NCH + c)
                    if c == 0:
                        gather(g - 1)
                    if c == 1:
                        complete(g - 1)
                    if c == 3:
                        residual(g - 1)
                    if c == 5:
                        normal(g - 1)
            gather(NG - 1)
            complete(NG - 1)
            residual(NG - 1)
            normal(NG - 1)
            for n in range(NG):
                i = (n + SPILL) % NG
                dve.wait_ge(y_made, n + 1)
                for b in range(NB):
                    v.tensor_tensor(tt[:, b * F:(b + 1) * F], aux[n % 2][:, b * F:(b + 1) * F], b1[:, :],
                                    ALU.add).then_inc(y_used, 1)
                    dve.wait_ge(y_used, n * NB + b + 1)
                    xb = x[:, i * IG + b * F:i * IG + (b + 1) * F]
                    v.scalar_tensor_tensor(xb, tt[:, b * F:(b + 1) * F], 0.0, xb, ALU.max,
                                           ALU.add).then_inc(o_made, 1)

        @block.tensor
        def _(pe):
            mm = nc.tensor.matmul
            chunks_due = pe.alloc_register("chunks_due")
            pe.reg_mov(chunks_due, NCH + 1)
            banks_due = pe.alloc_register("banks_due")
            pe.reg_mov(banks_due, 1)
            pe.wait_ge(w_here, 80)
            pe.wait_ge(row_made, 2)
            mm(aux[3][:, 0:2], w0[:, :], a2[:, :], start=True, stop=True).then_inc(wa_summed, 1)
            pe.wait_ge(ident_made, 1)
            for g in range(NG):
                pe.wait_ge(hn_made, g // 2 + 1)
                if g >= 2:
                    pe.wait_ge(act_pro, XQ + g - 1)
                for b in range(NB):
                    j = g * NB + b
                    last = nc.tensor.transpose(aux[g % 2][:, b * P:(b + 1) * P], hn[:, j * F:(j + 1) * F],
                                               ident[:, :])
                last.then_inc(pe_pro, 1)
            pe.wait_ge(dve_pro, XQ + 1)
            for g in range(NG):
                pe.wait_ge(act_pro, XQ + g + 1)
                for b in range(NB):
                    j = g * NB + b
                    last = mm(aux[3][:, 64 + 2 * j:66 + 2 * j], hT[:, j * P:(j + 1) * P], wa[:, :],
                              start=True, stop=True, skip_group_check=True)
            last.then_inc(cols_summed, 1)
            pe.wait_ge(dve_pro, XQ + 5)
            nc.tensor.transpose(aux[2][0:1, 0:P], smx[:, :], ident[:, :]).then_inc(smax_turned, 1)
            pe.wait_ge(dve_pro, XQ + 6)
            mm(aux[2][:, P:P + 1], ones[0:1, :], s1[0:1, 0:1], start=True, stop=True,
               skip_group_check=True).then_inc(smax_spread, 1)
            for g in range(NG):
                if g >= 2:
                    pe.wait_ge(row_made, 2 + g - 1)
                mm(acc[g % 2][:, :], wrow[:, :], hT[:, g * IG:(g + 1) * IG], start=True,
                   stop=True).then_inc(row_summed, 1)

            def chunk(g, c, t):
                o = (c % 2) * CH
                if isinstance(t, int):
                    pe.wait_ge(neg_made, t + 1)
                else:
                    wait_next(pe, neg_made, chunks_due, 1)
                for b in range(NB):
                    if c == 0:
                        if isinstance(t, int):
                            if b == 0:
                                pe.wait_ge(row_made, 2 + NG)
                        else:
                            wait_next(pe, u_made, banks_due, 1)
                    for k in range(CJ):
                        j = c * CJ + k
                        if isinstance(t, int) and b == 0:
                            pe.wait_ge(xab_made, j + 1)
                        first, end = j == 0, j == NJ - 1
                        q = o + k * IG + b * P
                        dp = pos[:, q:q + P].bitcast(F8)
                        dn = neg[:, q:q + P].bitcast(F8)
                        mm(acc[b][:, 0:2 * W], dp, XA[:, j, :, :].rearrange("p k w -> p (k w)"),
                           start=first, stop=end, skip_group_check=True)
                        mm(acc[b][:, 2 * W:3 * W], dn, XB[:, j, 0, :], start=False, stop=False,
                           skip_group_check=True)
                        last = mm(acc[b][:, 2 * W:3 * W], dn, XB[:, j, 1, :], start=False, stop=end,
                                  skip_group_check=True)
                    last.then_inc(block_summed, 1)

            def turn(g):
                pe.wait_ge(u_whole, g + 1)
                for b in range(NB):
                    last = nc.tensor.transpose(aux[2][:, b * P:(b + 1) * P], u[:, b * W:b * W + F], ident[:, :])
                last.then_inc(u_turned, 1)

            def project(g):
                pe.wait_ge(ut_here, g + 1)
                for b in range(NB):
                    last = mm(aux[3][:, b * F:(b + 1) * F], uT[:, b * P:(b + 1) * P], w0t[:, :],
                              start=True, stop=True, skip_group_check=True)
                last.then_inc(att_made, 1)

            for c in range(NCH):
                chunk(0, c, c)
                if c == 2:
                    pe.wait_ge(lone_made, 2)
                    mm(aux[0][:, 0:F], hrow[:, :], ident[:, :], start=True, stop=True).then_inc(lone_summed, 1)
            with pe.Fori(1, NG) as g:
                for c in range(NCH):
                    chunk(g, c, g * NCH + c)
                    if c == 1:
                        turn(g - 1)
                    if c == 3:
                        project(g - 1)
            turn(NG - 1)
            project(NG - 1)

            def project_y(n):
                pe.wait_ge(agg_here, n + 1)
                if n >= 2:
                    pe.wait_ge(o_made, (n - 1) * NB)
                for b in range(NB):
                    last = mm(aux[n % 2][:, b * F:(b + 1) * F], uT[:, b * P:(b + 1) * P], w1[:, :],
                              start=True, stop=True, skip_group_check=True)
                last.then_inc(y_made, 1)

            for n in range(NG):
                i = (n + SPILL) % NG
                if i < SPILL:
                    pe.wait_ge(back, 16 * SPILL)
                if n >= 2:
                    pe.wait_ge(agg_here, n - 1)
                if n == 0:
                    pe.wait_ge(u_made, NG * NB)
                for j in range(NJ):
                    if n == 0 and j % NB == 0:
                        pe.wait_ge(h2_made, j // NB + 1)
                    src = back_of(i) if i < SPILL else M[:, (i % SLOTS) * NJ * IG:(i % SLOTS + 1) * NJ * IG]
                    for k in range(2):
                        last = mm(acc[n % 2][:, :], h2[:, (2 * j + k) * F:(2 * j + k + 1) * F],
                                  src[:, j * IG:(j + 1) * IG].bitcast(F8),
                                  start=(j == 0 and k == 0), stop=(j == NJ - 1 and k == 1))
                    if j == 3 and n >= 1:
                        project_y(n - 1)
                last.then_inc(agg_summed, 1)
            project_y(NG - 1)


def kernel(x, adj, L0_gnn_W, L0_gnn_a, L1_gnn_W, L1_gnn_b):
    import numpy as np
    import concourse.bacc as bacc
    from concourse.bass_utils import run_bass_kernel_spmd

    def flat(a):
        return np.ascontiguousarray(a)

    x, adj, w0, a, w1, b1 = (np.asarray(t) for t in (x, adj, L0_gnn_W, L0_gnn_a, L1_gnn_W, L1_gnn_b))
    arrays = {
        "x_dram": flat(x.reshape(NJ, P, F).transpose(1, 0, 2)).reshape(P, NJ * F),
        "adj_dram": flat(adj.T.reshape(NJ, P, NG, IG).transpose(2, 1, 0, 3)).reshape(NG * P, NJ * IG),
        "w0_dram": flat(w0),
        "w0t_dram": flat(w0.T),
        "a_dram": flat(a.reshape(2, F).T),
        "w1_dram": flat(w1),
        "b1_dram": flat(b1),
    }
    nc = bacc.Bacc("TRN2", target_bir_lowering=False, num_devices=1)
    args = [nc.dram_tensor(k, t.shape, mybir.dt.from_np(t.dtype), kind="ExternalInput").ap()
            for k, t in arrays.items()]
    out = nc.dram_tensor("out_dram", (P, NJ * F), F32, kind="ExternalOutput").ap()
    spill = nc.dram_tensor("spill_dram", (P, SPILL * NJ * IG), U8, kind="Internal").ap()
    gat_sum_kernel(nc, *args, out, spill)
    r = run_bass_kernel_spmd(nc, [arrays], core_ids=[0])
    got = r.results[0]["out_dram"]
    return flat(got.reshape(P, NJ, F).transpose(1, 0, 2)).reshape(N, F)
```

```python
from contextlib import ExitStack

import concourse.bass as bass
from concourse import mybir

ALU = mybir.AluOpType
ACT = mybir.ActivationFunctionType
F32 = mybir.dt.float32
F16 = mybir.dt.float16
F8 = mybir.dt.float8e4
U8 = mybir.dt.uint8
U32 = mybir.dt.uint32
I32 = mybir.dt.int32
AX_X = mybir.AxisListType.X

P = 128
N = 4096
F = 128
NJ = N // P
IG = 512
NG = N // IG
NB = IG // P
CJ = 4
NCH = NJ // CJ
HJ = 2
RAW = 4
CH = CJ * IG
SLOTS = 5
SPILL = NG - SLOTS
ONE = 0x38
SC = 4096.0
EPS = 1e-5
W = F + 1
XQ = 4
QB = NJ // XQ
KACT = 1
BIG = 2.0 ** 120


def ds(start, size):
    return bass.ds(start, size)


def wait_next(eng, sem, level, step):
    eng.wait_ge(sem, level)
    eng.reg_add(level, level, step)


def gat_sum_kernel(nc, x_in, adj_in, w0_in, w0t_in, a_in, w1_in, b1_in, out, spill):
    with ExitStack() as ctx:
        def sb(name, shape, dt):
            return ctx.enter_context(nc.sbuf_tensor(name, shape, dt))

        def ps(name):
            return ctx.enter_context(nc.psum_tensor(name, [P, 512], F32))

        def sem(name):
            return ctx.enter_context(nc.semaphore(name))

        M = sb("M", [P, SLOTS * NJ * IG], U8)
        raw = sb("raw", [P, RAW * HJ * IG], I32)
        key = sb("key", [P, 2 * CH], U8)
        pos = sb("pos", [P, 2 * CH], U8)
        neg = sb("neg", [P, 2 * CH], U8)
        s_row = sb("s_row", [P, N], F32)
        s_now = sb("s_now", [P, IG], F32)
        XAB = sb("XAB", [P, 2 * NJ * 2 * W], F16)
        XA = XAB[:, 0:NJ * 2 * W].rearrange("p (j k w) -> p j k w", k=2, w=W)
        XB = XAB[:, NJ * 2 * W:].rearrange("p (j k w) -> p j k w", k=2, w=W)
        h2 = sb("h2", [P, NJ * 2 * F], F16)
        x = sb("x", [P, NJ * F], F32)
        ident = sb("ident", [P, P], F32)
        ones = sb("ones", [P, P], F32)
        w0 = sb("w0", [P, F], F32)
        w0t = sb("w0t", [P, F], F32)
        w1 = sb("w1", [P, F], F32)
        b1 = sb("b1", [P, F], F32)
        a2 = sb("a2", [P, 2], F32)
        wa = sb("wa", [P, 2], F32)
        wrow = sb("wrow", [P, P], F32)
        st = sb("st", [P, NJ * 6], F32)
        mv = sb("mv", [P, NJ * 2], F32)
        ve = sb("ve", [P, NJ], F32)
        rs = sb("rs", [P, NJ], F32)
        nm = sb("nm", [P, NJ], F32)
        nr = sb("nr", [P, NJ], F32)
        half = sb("half", [P, QB], F32)
        s_cols = sb("s_cols", [P, NJ, 2], F32)
        nsj = sb("nsj", [P, NJ], F32)
        smx = sb("smx", [P, 1], F32)
        s1 = sb("s1", [1, 1], F32)
        S = sb("S", [P, 1], F32)
        bsj = sb("bsj", [P, NJ], F32)
        et = sb("et", [P, 3 * NJ], F32)
        Fs = sb("Fs", [P, 2 * NJ], F32)
        Es = sb("Es", [P, 2 * NJ], F32)
        lone = sb("lone", [P, W], F32)
        u = sb("u", [P, NB * W], F32)
        uT = sb("uT", [P, IG], F32)
        z = sb("z", [P, NB], F32)
        rv = sb("rv", [P, NB], F32)
        gst = sb("gst", [P, NB * 6], F32)
        gmv = sb("gmv", [P, NB * 2], F32)
        gve = sb("gve", [P, NB], F32)
        grs = sb("grs", [P, NB], F32)
        gnm = sb("gnm", [P, NB], F32)
        tt = sb("tt", [P, NB * F], F32)
        hnb = M[:, (SLOTS - 1) * NJ * IG:SLOTS * NJ * IG].bitcast(F32)
        hn = hnb
        hT = M[:, (SLOTS - 2) * NJ * IG:(SLOTS - 1) * NJ * IG].bitcast(F32)

        acc = [ps(f"acc{b}") for b in range(NB)]
        aux = [ps(f"aux{b}") for b in range(4)]

        x_here = [sem(f"x_here{q}") for q in range(XQ)]
        w_here = sem("w_here")
        w0_here = sem("w0_here")
        raw_here = [sem(f"raw_here{b}") for b in range(RAW)]
        slot_free = sem("slot_free")
        mask_made = sem("mask_made")
        spilled = sem("spilled")
        back = sem("back")
        stored = sem("stored")
        ident_zero = sem("ident_zero")
        ident_made = sem("ident_made")
        dve_pro = sem("dve_pro")
        consts = sem("consts")
        pool_pro = sem("pool_pro")
        x_stats = sem("x_stats")
        x_devs = sem("x_devs")
        ht_turned = sem("ht_turned")
        ht_made = sem("ht_made")
        exp_made = sem("exp_made")
        row_now = sem("row_now")
        act_keys = sem("act_keys")
        pool_epi = sem("pool_epi")
        devs_made = sem("devs_made")
        act_scaled = sem("act_scaled")
        act_high = sem("act_high")
        hn_made = sem("hn_made")
        row_made = sem("row_made")
        keys_made = sem("keys_made")
        pos_made = sem("pos_made")
        neg_made = sem("neg_made")
        block_summed = sem("block_summed")
        xab_made = sem("xab_made")
        u_high = sem("u_high")
        u_low = sem("u_low")
        u_made = sem("u_made")
        dve_epi = sem("dve_epi")
        u_whole = sem("u_whole")
        u_turned = sem("u_turned")
        ut_here = sem("ut_here")
        att_made = sem("att_made")
        x1_made = sem("x1_made")
        var_made = sem("var_made")
        h2_made = sem("h2_made")
        agg_summed = sem("agg_summed")
        agg_here = sem("agg_here")
        y_made = sem("y_made")
        y_used = sem("y_used")
        o_made = sem("o_made")

        var_pro = sem("var_pro")
        wa_summed = sem("wa_summed")
        cols_summed = sem("cols_summed")
        smax_turned = sem("smax_turned")
        smax_spread = sem("smax_spread")
        row_summed = sem("row_summed")
        f_made = sem("f_made")
        xab_high = sem("xab_high")
        lone_made = sem("lone_made")
        lone_summed = sem("lone_summed")
        PRO_MAX, PRO_BSJ, PRO_ONE, PRO_EXP, PRO_ES = 4, 5, 7, 9, 13
        EPI = 3
        freed = sb("freed", [P, 2], F32)
        mv3 = mv[:, :].rearrange("p (j k) -> p j k", k=2)
        gmv3 = gmv[:, :].rearrange("p (j k) -> p j k", k=2)

        def back_of(g):
            w = NJ * IG
            if g < 2:
                return XAB[:, :].bitcast(U8)[:, g * w:(g + 1) * w]
            return s_row[:, :].bitcast(U8)

        block = ctx.enter_context(nc.Block())

        @block.sync
        def _(sp):
            for q in range(XQ):
                w = QB * F
                sp.dma_start(x[:, q * w:(q + 1) * w], x_in[:, q * w:(q + 1) * w]).then_inc(x_here[q], 16)
            sp.dma_start(w0[:, :], w0_in).then_inc(w0_here, 16)
            sp.dma_start(a2[:, :], a_in).then_inc(w0_here, 16)

            def load(g, h):
                b = h % RAW
                sp.dma_start(raw[:, b * HJ * IG:(b + 1) * HJ * IG],
                             adj_in[ds(g * P, P), h * HJ * IG:(h + 1) * HJ * IG]).then_inc(raw_here[b], 16)

            for h in range(RAW):
                load(0, h)
            sp.dma_start(w0t[:, :], w0t_in).then_inc(w_here, 16)
            sp.dma_start(w1[:, :], w1_in).then_inc(w_here, 16)
            sp.dma_start(b1[:, :], b1_in.partition_broadcast(P)).then_inc(w_here, 16)
            for h in range(RAW, 2 * NCH):
                sp.wait_ge(mask_made, h - RAW + 1)
                load(0, h)
            with sp.Fori(1, NG) as g:
                for h in range(2 * NCH):
                    sp.wait_ge(mask_made, g * 2 * NCH + (h - RAW + 1))
                    load(g, h)
            for g in range(NG):
                sp.wait_ge(o_made, (g + 1) * NB)
                w = IG
                i = (g + SPILL) % NG
                sp.dma_start(out[:, i * w:(i + 1) * w], x[:, i * w:(i + 1) * w]).then_inc(stored, 16)
            sp.wait_ge(stored, 16 * NG)

        @block.gpsimd
        def _(pool):
            p = nc.gpsimd
            p.memset(half[:, :], -0.5).then_inc(consts, 1)
            p.memset(ones[:, :], 1.0).then_inc(consts, 1)
            p.memset(lone[:, F:W], float(N)).then_inc(consts, 1)
            p.memset(ident[:, :], 0.0).then_inc(consts, 1)
            pool.wait_ge(consts, 4)
            p.affine_select(out=ident[:, :], in_=ident[:, :], compare_op=ALU.not_equal, fill=1.0,
                            base=0, pattern=[[-1, P]], channel_multiplier=1).then_inc(ident_made, 1)
            p.memset(freed[:, 0:1], 0.0).then_inc(slot_free, SLOTS)

            for q in range(XQ):
                r = slice(q * QB, (q + 1) * QB)
                pool.wait_ge(x_stats, q + 1)
                p.tensor_scalar(ve[:, r], mv3[:, r, 1], EPS, 1.0, ALU.add, ALU.mult).then_inc(pool_pro, 1)
                p.tensor_scalar(nm[:, r], mv3[:, r, 0], -1.0, 0.0, ALU.mult, ALU.add).then_inc(pool_pro, 1)
                pool.wait_ge(pool_pro, 3 * q + 1)
                p.tensor_tensor(rs[:, r], ve[:, r], half[:, :], ALU.pow).then_inc(pool_pro, 1)
                pool.wait_ge(pool_pro, 3 * q + 3)
                p.tensor_tensor(nr[:, r], nm[:, r], rs[:, r], ALU.mult).then_inc(x_devs, 1)

            def spill_group(g):
                w = NJ * IG
                pool.wait_ge(mask_made, (g + 1) * 2 * NCH)
                pool.dma_start(spill[:, g * w:(g + 1) * w], M[:, g * w:(g + 1) * w]).then_inc(spilled, 16)

            def deviations(g):
                pool.wait_ge(var_made, g + 1)
                p.tensor_scalar(gve[:, :], gmv3[:, :, 1], EPS, 1.0, ALU.add, ALU.mult).then_inc(pool_epi, 1)
                p.tensor_scalar(gnm[:, :], gmv3[:, :, 0], -SC, 0.0, ALU.mult, ALU.add).then_inc(devs_made, 1)
                pool.wait_ge(pool_epi, g + 1)
                p.tensor_tensor(grs[:, :], gve[:, :], half[:, 0:NB], ALU.pow).then_inc(devs_made, 1)

            for g in range(SPILL):
                spill_group(g)
                deviations(g)
            pool.wait_ge(spilled, 16 * SPILL)
            pool.wait_ge(neg_made, SPILL * NCH)
            p.memset(freed[:, 1:2], 0.0).then_inc(slot_free, SPILL)
            for g in range(SPILL, NG - 1):
                deviations(g)
            pool.wait_ge(block_summed, NG * NCH * NB)
            for g in range(SPILL):
                w = NJ * IG
                pool.dma_start(back_of(g), spill[:, g * w:(g + 1) * w]).then_inc(back, 16)
            deviations(NG - 1)

        @block.scalar
        def _(act):
            a = nc.scalar.activation
            for q in range(XQ):
                act.wait_ge(x_devs, q + 1)
                for j in range(q * QB, (q + 1) * QB):
                    ins = a(hn[:, j * F:(j + 1) * F], x[:, j * F:(j + 1) * F], ACT.Relu,
                            bias=nr[:, j:j + 1], scale=rs[:, j:j + 1])
                    if j % NB == NB - 1:
                        ins.then_inc(hn_made, 1)

            def row(g):
                act.wait_ge(row_summed, g + 1)
                a(s_row[:, g * IG:(g + 1) * IG], aux[g % 2][:, :], ACT.Copy).then_inc(row_made, 1)

            def row_for_keys(g):
                a(s_now[:, :], s_row[:, ds(g * IG, IG)], ACT.Copy).then_inc(row_now, 1)

            def keys_free(g, c, t):
                if c == 0:
                    act.wait_ge(row_now, g + 1)
                if not (isinstance(t, int) and t < 2):
                    act.wait_ge(neg_made, t - 1)

            def keys(c):
                o = (c % 2) * CH
                for k in range(KACT):
                    j = c * CJ + k
                    last = a(key[:, o + k * IG:o + (k + 1) * IG].bitcast(F8), s_now[:, :], ACT.Relu,
                             bias=bsj[:, j:j + 1], scale=BIG, saturate=False)
                last.then_inc(act_keys, 1)

            def masks(g, c):
                for k in range(2):
                    h = 2 * c + k
                    b = h % RAW
                    act.wait_ge(raw_here[b], 16 * (g * (2 * NCH // RAW) + h // RAW + 1))
                    a(M[:, ds((g % SLOTS) * (NJ * IG) + h * HJ * IG, HJ * IG)],
                      raw[:, b * HJ * IG:(b + 1) * HJ * IG],
                      ACT.Copy, scale=float(ONE)).then_inc(mask_made, 1)

            def high_parts(g):
                for b in range(NB):
                    act.wait_ge(block_summed, g * (NCH * NB) + ((NCH - 1) * NB + b + 1))
                    a(u[:, b * W:(b + 1) * W], acc[b][:, 0:W], ACT.Copy,
                      scale=Es[:, ds(g * NB + b, 1)]).then_inc(u_high, 1)

            def turned(g):
                act.wait_ge(u_turned, g + 1)
                a(uT[:, :], aux[2][:, :], ACT.Copy).then_inc(ut_here, 1)

            def centred(g):
                act.wait_ge(devs_made, 2 * g + 2)
                for b in range(NB):
                    last = a(tt[:, b * F:(b + 1) * F], x[:, ds(g * IG + b * F, F)], ACT.Relu,
                             bias=gnm[:, b:b + 1], scale=SC)
                last.then_inc(act_scaled, 1)
                act.wait_ge(act_scaled, g + 1)
                for b in range(NB):
                    last = a(h2[:, ds(g * 2 * IG + 2 * b * F, F)], tt[:, b * F:(b + 1) * F], ACT.Copy,
                             scale=grs[:, b:b + 1])
                last.then_inc(act_high, 1)

            def weighted(j):
                for k, X in enumerate((XA, XB)):
                    last = a(X[:, j, 0, 0:F], hn[:, j * F:(j + 1) * F], ACT.Copy,
                             scale=Fs[:, k * NJ + j:k * NJ + j + 1])
                last.then_inc(xab_high, 1)

            row(0)
            act.wait_ge(row_made, 1)
            row_for_keys(0)
            act.wait_ge(dve_pro, PRO_BSJ)
            keys_free(0, 0, 0)
            keys(0)
            masks(0, 0)
            act.wait_ge(dve_pro, PRO_EXP)
            a(Fs[:, 0:NJ], et[:, 0:NJ], ACT.Exp).then_inc(exp_made, 1)
            a(Fs[:, NJ:], et[:, 0:NJ], ACT.Exp, scale=0.2).then_inc(exp_made, 1)
            act.wait_ge(f_made, 1)
            for c in range(NCH):
                for k in range(CJ):
                    weighted(c * CJ + k)
                if c == 0:
                    act.wait_ge(dve_pro, PRO_ES)
                    a(Es[:, :], et[:, NJ:3 * NJ], ACT.Exp).then_inc(exp_made, 1)
                if c >= 1:
                    keys_free(0, c, c)
                    masks(0, c)
                    keys(c)
                    row(c)
            act.wait_ge(row_made, NG)
            with act.Fori(1, NG) as g:
                act.wait_ge(slot_free, g + 1)
                row_for_keys(g)
                for c in range(NCH):
                    keys_free(g, c, g * NCH + c)
                    masks(g, c)
                    keys(c)
                    if c == 1:
                        high_parts(g - 1)
                    if c == 3:
                        turned(g - 1)
                    if c == 7:
                        centred(g - 1)
            high_parts(NG - 1)
            turned(NG - 1)
            centred(NG - 1)
            for n in range(NG):
                act.wait_ge(agg_summed, n + 1)
                if n >= 1:
                    act.wait_ge(y_made, n)
                a(uT[:, :], aux[n % 2][:, :], ACT.Copy, scale=1.0 / SC).then_inc(agg_here, 1)

        @block.vector
        def _(dve):
            v = nc.vector
            x1_due = dve.alloc_register("x1_due")
            dve.reg_mov(x1_due, 1)
            stats_due = dve.alloc_register("stats_due")
            dve.reg_mov(stats_due, 3)
            n = [0]

            def step(ins):
                n[0] += 1
                ins.then_inc(dve_pro, 1)

            def settle():
                dve.wait_ge(dve_pro, n[0])

            dve.wait_ge(wa_summed, 1)
            step(v.tensor_copy(wa[:, :], aux[3][:, 0:2]))
            settle()
            step(v.tensor_copy(wrow[:, :], wa[:, 0:1].to_broadcast([P, P])))

            def statistics(q):
                dve.wait_ge(x_here[q], 16)
                for j in range(q * QB, (q + 1) * QB):
                    last = v.bn_stats(st[:, j * 6:(j + 1) * 6], x[:, j * F:(j + 1) * F])
                last.then_inc(var_pro, 1)
                dve.wait_ge(var_pro, q + 1)
                for j in range(q * QB, (q + 1) * QB):
                    last = v.bn_aggr(mv[:, 2 * j:2 * j + 2], st[:, j * 6:(j + 1) * 6])
                last.then_inc(x_stats, 1)

            def transposed(g):
                dve.wait_ge(ht_turned, g + 1)
                v.tensor_copy(hT[:, g * IG:(g + 1) * IG], acc[g % 2][:, :]).then_inc(ht_made, 1)

            for q in range(XQ - 1):
                statistics(q)
            transposed(0)
            transposed(1)
            statistics(XQ - 1)
            for g in range(2, NG):
                transposed(g)
            dve.wait_ge(cols_summed, 1)
            step(v.tensor_copy(s_cols[:, :, :].rearrange("p j k -> p (j k)"), aux[3][:, 64:64 + 2 * NJ]))
            settle()
            step(v.reduce_max(smx[:, :], s_cols[:, :, 1], AX_X))
            assert n[0] == PRO_MAX
            step(v.tensor_scalar(bsj[:, :], s_cols[:, :, 1], BIG, None, ALU.mult))
            assert n[0] == PRO_BSJ
            step(v.tensor_scalar(nsj[:, :], s_cols[:, :, 1], -1.0, None, ALU.mult))
            dve.wait_ge(smax_turned, 1)
            step(v.reduce_max(s1[:, :], aux[2][0:1, 0:P], AX_X))
            assert n[0] == PRO_ONE
            dve.wait_ge(row_made, 1)
            settle()

            def keys(g, c, t):
                o = (c % 2) * CH
                for k in range(KACT, CJ):
                    j = c * CJ + k
                    last = v.tensor_scalar(key[:, o + k * IG:o + (k + 1) * IG], s_row[:, ds(g * IG, IG)],
                                           nsj[:, j:j + 1], float(ONE), ALU.is_gt, ALU.mult)
                last.then_inc(keys_made, 1)

            keys(0, 0, 0)
            dve.wait_ge(smax_spread, 1)
            step(v.tensor_copy(S[:, 0:1], aux[2][:, P:P + 1]))
            settle()
            step(v.tensor_scalar(et[:, 0:NJ], s_cols[:, :, 1], S[:, 0:1], None, ALU.subtract))
            assert n[0] == PRO_EXP
            step(v.tensor_scalar(et[:, NJ:2 * NJ], s_cols[:, :, 0], S[:, 0:1], None, ALU.add))
            settle()
            step(v.scalar_tensor_tensor(tt[:, 0:NJ], et[:, NJ:2 * NJ], 0.2, et[:, NJ:2 * NJ], ALU.mult, ALU.max))
            settle()
            step(v.scalar_tensor_tensor(et[:, 2 * NJ:], et[:, NJ:2 * NJ], 0.2, tt[:, 0:NJ], ALU.mult, ALU.subtract))
            settle()
            step(v.tensor_tensor(et[:, NJ:2 * NJ], et[:, NJ:2 * NJ], tt[:, 0:NJ], ALU.subtract))
            assert n[0] == PRO_ES
            dve.wait_ge(exp_made, 2)
            v.tensor_scalar(Fs[:, :], Fs[:, :], SC, None, ALU.mult).then_inc(f_made, 1)
            dve.wait_ge(f_made, 1)
            for k, X in enumerate((XA, XB)):
                fk = Fs[:, k * NJ:(k + 1) * NJ]
                v.tensor_copy(X[:, :, 0, F], fk).then_inc(f_made, 1)
                dve.wait_ge(f_made, 2 + 2 * k)
                v.tensor_tensor(X[:, :, 1, F], fk, X[:, :, 0, F], ALU.subtract).then_inc(f_made, 1)

            def low_parts(j):
                h = hn[:, j * F:(j + 1) * F]
                dve.wait_ge(xab_high, j + 1)
                for k, X in enumerate((XA, XB)):
                    last = v.scalar_tensor_tensor(X[:, j, 1, 0:F], h, Fs[:, k * NJ + j:k * NJ + j + 1],
                                                  X[:, j, 0, 0:F], ALU.mult, ALU.subtract)
                last.then_inc(xab_made, 1)

            def split(g, c, t):
                o = (c % 2) * CH
                m = M[:, ds((g % SLOTS) * (NJ * IG) + c * CH, CH)].bitcast(U32)
                dve.wait_ge(mask_made, t * 2 + 2)
                dve.wait_ge(act_keys, t + 1)
                if not (isinstance(t, int) and t < 2):
                    dve.wait_ge(block_summed, (t - 1) * NB)
                dve.wait_ge(keys_made, t + 1)
                v.tensor_tensor(pos[:, o:o + CH].bitcast(U32), m, key[:, o:o + CH].bitcast(U32),
                                ALU.bitwise_and).then_inc(pos_made, 1)
                dve.wait_ge(pos_made, t + 1)
                v.tensor_tensor(neg[:, o:o + CH].bitcast(U32), m, pos[:, o:o + CH].bitcast(U32),
                                ALU.bitwise_xor).then_inc(neg_made, 1)

            def gather(g):
                for b in range(NB):
                    dve.wait_ge(u_high, g * NB + b + 1)
                    ub = u[:, b * W:(b + 1) * W]
                    v.scalar_tensor_tensor(ub, acc[b][:, W:2 * W], Es[:, ds(g * NB + b, 1)], ub,
                                           ALU.mult, ALU.add).then_inc(u_low, 1)
                    dve.wait_ge(u_low, g * NB + b + 1)
                    v.scalar_tensor_tensor(ub, acc[b][:, 2 * W:3 * W], Es[:, ds(g * NB + (NJ + b), 1)], ub,
                                           ALU.mult, ALU.add).then_inc(u_made, 1)

            def complete(g):
                uw = u[:, :].rearrange("p (b w) -> p b w", w=W)
                dve.wait_ge(u_made, g * NB + NB)
                v.tensor_scalar(z[:, :], uw[:, :, F], 0.0, None, ALU.is_equal).then_inc(dve_epi, 1)
                dve.wait_ge(dve_epi, g * EPI + 1)
                for b in range(NB):
                    ub = u[:, b * W:(b + 1) * W]
                    last = v.scalar_tensor_tensor(ub, lone[:, :], z[:, b:b + 1], ub, ALU.mult, ALU.add)
                last.then_inc(u_whole, 1)
                dve.wait_ge(u_whole, g + 1)
                v.reciprocal(rv[:, :], uw[:, :, F]).then_inc(dve_epi, 1)

            def residual(g):
                dve.wait_ge(att_made, g + 1)
                dve.wait_ge(dve_epi, g * EPI + 2)
                for b in range(NB):
                    xb = x[:, ds(g * IG + b * F, F)]
                    last = v.scalar_tensor_tensor(xb, aux[3][:, b * F:(b + 1) * F], rv[:, b:b + 1], xb,
                                                  ALU.mult, ALU.add)
                last.then_inc(x1_made, 1)
                if isinstance(g, int):
                    dve.wait_ge(x1_made, g + 1)
                else:
                    wait_next(dve, x1_made, x1_due, 1)
                for b in range(NB):
                    last = v.bn_stats(gst[:, b * 6:(b + 1) * 6], x[:, ds(g * IG + b * F, F)])
                last.then_inc(dve_epi, 1)
                if isinstance(g, int):
                    dve.wait_ge(dve_epi, g * EPI + 3)
                else:
                    wait_next(dve, dve_epi, stats_due, EPI)
                for b in range(NB):
                    last = v.bn_aggr(gmv[:, 2 * b:2 * b + 2], gst[:, b * 6:(b + 1) * 6])
                last.then_inc(var_made, 1)

            def low_normal(g):
                dve.wait_ge(act_high, g + 1)
                for b in range(NB):
                    last = v.scalar_tensor_tensor(h2[:, ds(g * 2 * IG + (2 * b + 1) * F, F)],
                                                  tt[:, b * F:(b + 1) * F], grs[:, b:b + 1],
                                                  h2[:, ds(g * 2 * IG + 2 * b * F, F)],
                                                  ALU.mult, ALU.subtract)
                last.then_inc(h2_made, 1)

            for c in range(NCH):
                if c >= 1:
                    keys(0, c, c)
                for k in range(CJ):
                    low_parts(c * CJ + k)
                split(0, c, c)
            dve.wait_ge(lone_summed, 1)
            v.tensor_reduce(lone[:, 0:F], aux[2][:, :].rearrange("p (b f) -> p f b", f=F), AX_X,
                            ALU.add).then_inc(lone_made, 1)
            dve.wait_ge(lone_made, 1)
            with dve.Fori(1, NG) as g:
                keys(g, 0, g * NCH)
                for c in range(NCH):
                    t = g * NCH + c
                    if c + 1 < NCH:
                        keys(g, c + 1, t + 1)
                    split(g, c, t)
                    if c == 0:
                        gather(g - 1)
                    if c == 1:
                        complete(g - 1)
                    if c == 5:
                        residual(g - 1)
                low_normal(g - 1)
            gather(NG - 1)
            complete(NG - 1)
            residual(NG - 1)
            low_normal(NG - 1)
            dve.wait_ge(w_here, 48)
            for n in range(NG):
                i = (n + SPILL) % NG
                dve.wait_ge(y_made, n + 1)
                if n >= 1:
                    dve.wait_ge(o_made, n * NB)
                for b in range(NB):
                    v.tensor_tensor(tt[:, b * F:(b + 1) * F], acc[n % 2][:, b * F:(b + 1) * F], b1[:, :],
                                    ALU.add).then_inc(y_used, 1)
                for b in range(NB):
                    dve.wait_ge(y_used, n * NB + b + 1)
                    xb = x[:, i * IG + b * F:i * IG + (b + 1) * F]
                    v.scalar_tensor_tensor(xb, tt[:, b * F:(b + 1) * F], 0.0, xb, ALU.max,
                                           ALU.add).then_inc(o_made, 1)

        @block.tensor
        def _(pe):
            mm = nc.tensor.matmul
            chunks_due = pe.alloc_register("chunks_due")
            pe.reg_mov(chunks_due, NCH + 1)
            banks_due = pe.alloc_register("banks_due")
            pe.reg_mov(banks_due, 1)
            pe.wait_ge(w0_here, 32)
            mm(aux[3][:, 0:2], w0[:, :], a2[:, :], start=True, stop=True).then_inc(wa_summed, 1)

            def row(g):
                if g >= 2:
                    pe.wait_ge(row_made, g - 1)
                mm(aux[g % 2][:, :], wrow[:, :], hT[:, g * IG:(g + 1) * IG], start=True,
                   stop=True).then_inc(row_summed, 1)

            def turn_x(g):
                pe.wait_ge(hn_made, g + 1)
                if g >= 2:
                    pe.wait_ge(ht_made, g - 1)
                for b in range(NB):
                    j = g * NB + b
                    last = nc.tensor.transpose(acc[g % 2][:, b * P:(b + 1) * P], hn[:, j * F:(j + 1) * F],
                                               ident[:, :])
                last.then_inc(ht_turned, 1)

            def cols(g):
                pe.wait_ge(ht_made, g + 1)
                for b in range(NB):
                    j = g * NB + b
                    last = mm(aux[3][:, 64 + 2 * j:66 + 2 * j], hT[:, j * P:(j + 1) * P], wa[:, :],
                              start=True, stop=True, skip_group_check=True)
                return last

            pe.wait_ge(ident_made, 1)
            turn_x(0)
            pe.wait_ge(dve_pro, 2)
            for g in range(1, NG):
                turn_x(g)
                cols(g - 1)
            cols(NG - 1).then_inc(cols_summed, 1)
            row(0)
            pe.wait_ge(dve_pro, PRO_MAX)
            nc.tensor.transpose(aux[2][0:1, 0:P], smx[:, :], ident[:, :]).then_inc(smax_turned, 1)
            pe.wait_ge(dve_pro, PRO_ONE)
            mm(aux[2][:, P:P + 1], ones[0:1, :], s1[0:1, 0:1], start=True, stop=True,
               skip_group_check=True).then_inc(smax_spread, 1)

            def chunk(g, c, t):
                o = (c % 2) * CH
                if isinstance(t, int):
                    pe.wait_ge(neg_made, t + 1)
                else:
                    wait_next(pe, neg_made, chunks_due, 1)
                for b in range(NB):
                    if c == 0:
                        if not isinstance(t, int):
                            wait_next(pe, u_made, banks_due, 1)
                    for k in range(CJ):
                        j = c * CJ + k
                        if isinstance(t, int) and b == 0:
                            pe.wait_ge(xab_made, j + 1)
                        first, end = j == 0, j == NJ - 1
                        q = o + k * IG + b * P
                        dp = pos[:, q:q + P].bitcast(F8)
                        dn = neg[:, q:q + P].bitcast(F8)
                        mm(acc[b][:, 0:2 * W], dp, XA[:, j, :, :].rearrange("p k w -> p (k w)"),
                           start=first, stop=end, skip_group_check=True)
                        mm(acc[b][:, 2 * W:3 * W], dn, XB[:, j, 0, :], start=False, stop=False,
                           skip_group_check=True)
                        last = mm(acc[b][:, 2 * W:3 * W], dn, XB[:, j, 1, :], start=False, stop=end,
                                  skip_group_check=True)
                    last.then_inc(block_summed, 1)

            def turn(g):
                pe.wait_ge(u_whole, g + 1)
                for b in range(NB):
                    last = nc.tensor.transpose(aux[2][:, b * P:(b + 1) * P], u[:, b * W:b * W + F], ident[:, :])
                last.then_inc(u_turned, 1)

            def project(g):
                pe.wait_ge(ut_here, g + 1)
                for b in range(NB):
                    last = mm(aux[3][:, b * F:(b + 1) * F], uT[:, b * P:(b + 1) * P], w0t[:, :],
                              start=True, stop=True, skip_group_check=True)
                last.then_inc(att_made, 1)

            for c in range(NCH):
                chunk(0, c, c)
                if c + 1 < NG:
                    row(c + 1)
            pe.wait_ge(dve_pro, PRO_ES)
            for g in range(NG):
                last = mm(aux[2][:, :], ones[:, :], hn[:, g * IG:(g + 1) * IG], start=(g == 0),
                          stop=(g == NG - 1))
            last.then_inc(lone_summed, 1)
            pe.wait_ge(w_here, 48)
            with pe.Fori(1, NG) as g:
                for c in range(NCH):
                    chunk(g, c, g * NCH + c)
                    if c == 1:
                        turn(g - 1)
                    if c == 3:
                        project(g - 1)

            def project_y(n):
                pe.wait_ge(agg_here, n + 1)
                if n >= 2:
                    pe.wait_ge(o_made, (n - 1) * NB)
                for b in range(NB):
                    last = mm(acc[n % 2][:, b * F:(b + 1) * F], uT[:, b * P:(b + 1) * P], w1[:, :],
                              start=True, stop=True, skip_group_check=True)
                last.then_inc(y_made, 1)

            for n in range(NG):
                i = (n + SPILL) % NG
                if i < SPILL:
                    pe.wait_ge(back, 16 * SPILL)
                if n >= 2:
                    pe.wait_ge(agg_here, n - 1)
                for j in range(NJ):
                    if n == 0 and j % NB == 0:
                        pe.wait_ge(h2_made, j // NB + 1)
                    src = back_of(i) if i < SPILL else M[:, (i % SLOTS) * NJ * IG:(i % SLOTS + 1) * NJ * IG]
                    for k in range(2):
                        last = mm(aux[n % 2][:, :], h2[:, (2 * j + k) * F:(2 * j + k + 1) * F],
                                  src[:, j * IG:(j + 1) * IG].bitcast(F8),
                                  start=(j == 0 and k == 0), stop=(j == NJ - 1 and k == 1))
                    if n == 0 and j == 7:
                        turn(NG - 1)
                    if n == 0 and j == 15:
                        project(NG - 1)
                    if j == 3 and n >= 1:
                        project_y(n - 1)
                last.then_inc(agg_summed, 1)
            project_y(NG - 1)


def kernel(x, adj, L0_gnn_W, L0_gnn_a, L1_gnn_W, L1_gnn_b):
    import numpy as np
    import concourse.bacc as bacc
    from concourse.bass_utils import run_bass_kernel_spmd

    def flat(a):
        return np.ascontiguousarray(a)

    x, adj, w0, a, w1, b1 = (np.asarray(t) for t in (x, adj, L0_gnn_W, L0_gnn_a, L1_gnn_W, L1_gnn_b))
    arrays = {
        "x_dram": flat(x.reshape(NJ, P, F).transpose(1, 0, 2)).reshape(P, NJ * F),
        "adj_dram": flat(adj.T.reshape(NJ, P, NG, IG).transpose(2, 1, 0, 3)).reshape(NG * P, NJ * IG),
        "w0_dram": flat(w0),
        "w0t_dram": flat(w0.T),
        "a_dram": flat(a.reshape(2, F).T),
        "w1_dram": flat(w1),
        "b1_dram": flat(b1),
    }
    nc = bacc.Bacc("TRN2", target_bir_lowering=False, num_devices=1)
    args = [nc.dram_tensor(k, t.shape, mybir.dt.from_np(t.dtype), kind="ExternalInput").ap()
            for k, t in arrays.items()]
    out = nc.dram_tensor("out_dram", (P, NJ * F), F32, kind="ExternalOutput").ap()
    spill = nc.dram_tensor("spill_dram", (P, SPILL * NJ * IG), U8, kind="Internal").ap()
    gat_sum_kernel(nc, *args, out, spill)
    r = run_bass_kernel_spmd(nc, [arrays], core_ids=[0])
    got = r.results[0]["out_dram"]
    return flat(got.reshape(P, NJ, F).transpose(1, 0, 2)).reshape(N, F)
```

```python
from contextlib import ExitStack

import concourse.bass as bass
from concourse import mybir

ALU = mybir.AluOpType
ACT = mybir.ActivationFunctionType
F32 = mybir.dt.float32
F16 = mybir.dt.float16
F8 = mybir.dt.float8e4
U8 = mybir.dt.uint8
U32 = mybir.dt.uint32
I32 = mybir.dt.int32
AX_X = mybir.AxisListType.X

P = 128
N = 4096
F = 128
NJ = N // P
IG = 512
NG = N // IG
NB = IG // P
CJ = 4
NCH = NJ // CJ
HJ = 2
RAW = 4
CH = CJ * IG
KEEP = NG // 2
SLOTS = KEEP + 1
MERGED = NG - 1 - KEEP
ONE = 0x38
TWO = 0x40
KEY = 0x78
ORDER = [KEEP - 1, NG - 1] + [g for m in range(MERGED) for g in (KEEP + m, m)]
ROUNDS = [(g, 0, NB) for g in ORDER[:-1]] + [(ORDER[-1], 0, 2), (ORDER[-1], 2, 1), (ORDER[-1], 3, 1)]
SC = 4096.0
EPS = 1e-5
W = F + 1
XQ = 4
QB = NJ // XQ
XH = 2 * XQ
HB = NJ // XH
HF = 4
NT = 3
KACT = 1
WARM = 4
SUMS_EARLY = 3
BIG = 2.0 ** 90


def ds(start, size):
    return bass.ds(start, size)


def blocks_before(r):
    return sum(nb for _, _, nb in ROUNDS[:r])


def wait_next(eng, sem, level, step):
    eng.wait_ge(sem, level)
    eng.reg_add(level, level, step)


def gat_sum_kernel(nc, x_in, adj_in, w0_in, w0t_in, a_in, w1_in, b1_in, out, s_dram):
    with ExitStack() as ctx:
        def sb(name, shape, dt):
            return ctx.enter_context(nc.sbuf_tensor(name, shape, dt))

        def ps(name):
            return ctx.enter_context(nc.psum_tensor(name, [P, 512], F32))

        def sem(name):
            return ctx.enter_context(nc.semaphore(name))

        M = sb("M", [P, SLOTS * NJ * IG], U8)
        raw = sb("raw", [P, RAW * HJ * IG], I32)
        key = sb("key", [P, 2 * CH], U8)
        pos = sb("pos", [P, 2 * CH], U8)
        neg = sb("neg", [P, 2 * CH], U8)
        s_row = sb("s_row", [P, N], F32)
        s_now = sb("s_now", [P, IG], F32)
        XAB = sb("XAB", [P, 2 * NJ * 2 * W], F16)
        XA = XAB[:, 0:NJ * 2 * W].rearrange("p (j k w) -> p j k w", k=2, w=W)
        XB = XAB[:, NJ * 2 * W:].rearrange("p (j k w) -> p j k w", k=2, w=W)
        h2 = sb("h2", [P, NJ * 2 * F], F16)
        x = sb("x", [P, NJ * F], F32)
        ident = sb("ident", [P, P], F32)
        ones = sb("ones", [P, P], F32)
        w0 = sb("w0", [P, F], F32)
        w0t = sb("w0t", [P, F], F32)
        w1 = sb("w1", [P, F], F32)
        b1 = sb("b1", [P, F], F32)
        a2 = sb("a2", [P, 2], F32)
        wa = sb("wa", [P, 2 * F + 2], F32)
        st = sb("st", [P, NJ * 6], F32)
        mv = sb("mv", [P, NJ * 2], F32)
        ve = sb("ve", [P, NJ], F32)
        rs = sb("rs", [P, NJ], F32)
        rsc = sb("rsc", [P, NJ], F32)
        nm = sb("nm", [P, NJ], F32)
        half = sb("half", [P, QB], F32)
        sj_raw = sb("sj_raw", [P, NJ], F32)
        s_cols = sb("s_cols", [P, 2 * NJ], F32)
        s_turned = sb("s_turned", [NT * NB, P], F32)
        si_squares = sb("si_squares", [P, NJ], F32)
        nsj = sb("nsj", [P, NJ], F32)
        smx = sb("smx", [P, 1], F32)
        S = sb("S", [P, 1], F32)
        bsj = sb("bsj", [P, NJ], F32)
        et = sb("et", [P, 3 * NJ], F32)
        Fs = sb("Fs", [P, 2 * NJ], F32)
        Gs = sb("Gs", [P, 2 * NJ], F32)
        Es = sb("Es", [P, 2 * NJ], F32)
        lone = sb("lone", [P, W], F32)
        u = sb("u", [P, NB * W], F32)
        uT = sb("uT", [P, IG], F32)
        z = sb("z", [P, NB], F32)
        rv = sb("rv", [P, NB], F32)
        gst = sb("gst", [P, NB * 6], F32)
        gmv = sb("gmv", [P, NB * 2], F32)
        gve = sb("gve", [P, NB], F32)
        grs = sb("grs", [P, NB], F32)
        gnm = sb("gnm", [P, NB], F32)
        tt = sb("tt", [P, NB * F], F32)
        hc = M[:, (SLOTS - 1) * NJ * IG:SLOTS * NJ * IG].bitcast(F32)
        work = M[:, (SLOTS - 2) * NJ * IG:(SLOTS - 1) * NJ * IG].bitcast(F32)
        hf = work[:, 0:HF * IG]
        hT = work[:, 0:NT * IG]
        hn4 = work[:, HF * IG:(HF + 1) * IG]
        hsum = work[:, (HF + 1) * IG:(HF + 2) * IG]
        products = work[:, (HF + 2) * IG:]

        acc = [ps(f"acc{b}") for b in range(NB)]
        aux = [ps(f"aux{b}") for b in range(4)]

        def sems(names):
            return [sem(n) for n in names.split()]

        x_here = [sem(f"x_here{h}") for h in range(XH)]
        raw_here = [sem(f"raw_here{b}") for b in range(RAW)]
        w_here, w0_here, a_here = sems("w_here w0_here a_here")
        consts, ident_made = sems("consts ident_made")
        stats_made, x_stats, nm_made, ve_made, x_devs, hc_made = sems(
            "stats_made x_stats nm_made ve_made x_devs hc_made")
        a_spread, wa_summed, wa_made = sems("a_spread wa_summed wa_made")
        ht_turned, ht_by_act, ht_by_dve, cols_summed, scores_made = sems(
            "ht_turned ht_by_act ht_by_dve cols_summed scores_made")
        si_made, si_turned, s_turned_made, row_summed, row_made = sems(
            "si_made si_turned s_turned_made row_summed row_made")
        si_added, si_late, si_squared, row_sent, row_here = sems("si_added si_late si_squared row_sent row_here")
        dve_steps, sj_made, smax_made, smax_spread, less_max = sems(
            "dve_steps sj_made smax_made smax_spread less_max")
        f_made, rsc_made, g_made, f_high, f_cols = sems("f_made rsc_made g_made f_high f_cols")
        hf_first, hf_made, xab_high, xab_made = sems("hf_first hf_made xab_high xab_made")
        hn4_made, hsum_made, lone_summed, lone_made = sems("hn4_made hsum_made lone_summed lone_made")
        e_steps, e_made = sems("e_steps e_made")
        mask_made, merged, row_now, act_keys, keys_made, pos_made, neg_made = sems(
            "mask_made merged row_now act_keys keys_made pos_made neg_made")
        block_summed, u_high, u_low, u_made = sems("block_summed u_high u_low u_made")
        dve_epi, u_whole, u_turned, ut_here, att_made, x1_made, var_made, pool_epi, devs_made = sems(
            "dve_epi u_whole u_turned ut_here att_made x1_made var_made pool_epi devs_made")
        act_scaled, act_high, h2_made = sems("act_scaled act_high h2_made")
        apart, agg_summed, agg_here, y_made, y_used, o_made, stored = sems(
            "apart agg_summed agg_here y_made y_used o_made stored")

        EPI = 3
        mv3 = mv[:, :].rearrange("p (j k) -> p j k", k=2)
        gmv3 = gmv[:, :].rearrange("p (j k) -> p j k", k=2)

        def slot(g, late):
            return KEEP * NJ * IG if late else g * (NJ * IG)

        def apart_of(m):
            w = NJ * IG
            return XAB[:, :].bitcast(U8)[:, m * w:(m + 1) * w] if m < 2 else s_row[:, :].bitcast(U8)

        block = ctx.enter_context(nc.Block())

        @block.sync
        def _(sp):
            for h in range(XH):
                w = HB * F
                sp.dma_start(x[:, h * w:(h + 1) * w], x_in[:, h * w:(h + 1) * w]).then_inc(x_here[h], 16)

            def load(g, h):
                b = h % RAW
                sp.dma_start(raw[:, b * HJ * IG:(b + 1) * HJ * IG],
                             adj_in[ds(g * P, P), h * HJ * IG:(h + 1) * HJ * IG]).then_inc(raw_here[b], 16)

            for h in range(RAW):
                load(0, h)
            sp.dma_start(w0t[:, :], w0t_in).then_inc(w_here, 16)
            sp.dma_start(w1[:, :], w1_in).then_inc(w_here, 16)
            sp.dma_start(b1[:, :], b1_in.partition_broadcast(P)).then_inc(w_here, 16)

            for h in range(RAW, 2 * NCH):
                sp.wait_ge(mask_made, h - RAW + 1)
                load(0, h)
            with sp.Fori(1, NG) as g:
                for h in range(2 * NCH):
                    sp.wait_ge(mask_made, g * 2 * NCH + (h - RAW + 1))
                    load(g, h)
            for r, (g, b0, nb) in enumerate(ROUNDS):
                sp.wait_ge(o_made, blocks_before(r + 1))
                cols = slice(g * IG + b0 * F, g * IG + (b0 + nb) * F)
                sp.dma_start(out[:, cols], x[:, cols]).then_inc(stored, 16)
            sp.wait_ge(stored, 16 * len(ROUNDS))

        @block.gpsimd
        def _(pool):
            p = nc.gpsimd
            p.memset(half[:, :], -0.5).then_inc(consts, 1)
            p.memset(ones[:, :], 1.0).then_inc(consts, 1)
            p.memset(lone[:, F:W], float(N)).then_inc(consts, 1)
            p.memset(ident[:, :], 0.0).then_inc(consts, 1)
            pool.wait_ge(consts, 4)
            p.affine_select(out=ident[:, :], in_=ident[:, :], compare_op=ALU.not_equal, fill=1.0,
                            base=0, pattern=[[-1, P]], channel_multiplier=1).then_inc(ident_made, 1)

            def x_deviations(q):
                r = slice(q * QB, (q + 1) * QB)
                pool.wait_ge(x_stats, q + 1)
                p.tensor_scalar(nm[:, r], mv3[:, r, 0], -1.0, 0.0, ALU.mult, ALU.add).then_inc(nm_made, 1)
                p.tensor_scalar(ve[:, r], mv3[:, r, 1], EPS, 1.0, ALU.add, ALU.mult).then_inc(ve_made, 1)
                pool.wait_ge(ve_made, q + 1)
                p.tensor_tensor(rs[:, r], ve[:, r], half[:, :], ALU.pow).then_inc(x_devs, 1)

            def four(t, c):
                return t[:, c * IG:(c + 1) * IG].rearrange("p (b f) -> p b f", f=F)

            def spread(t, o):
                return t[:, o:o + NB].unsqueeze(2).to_broadcast([P, NB, F])

            def sum_hn(c):
                pool.wait_ge(hc_made, c + 1)
                if c == 0:
                    p.tensor_tensor(four(hsum, 0), four(hc, 0), spread(rs, 0), ALU.mult).then_inc(hsum_made, 1)
                    return
                pool.wait_ge(hsum_made, c)
                p.tensor_tensor(four(hn4, 0), four(hc, c), spread(rs, c * NB), ALU.mult).then_inc(hn4_made, 1)
                pool.wait_ge(hn4_made, c)
                p.tensor_tensor(hsum, hsum, hn4, ALU.add).then_inc(hsum_made, 1)

            def scaled_f(m):
                c, k = divmod(m, 2)
                if m >= HF:
                    pool.wait_ge(xab_made, m - HF + 1)
                p.tensor_tensor(four(hf, m % HF), four(hc, c), spread(Gs, k * NJ + c * NB),
                                ALU.mult).then_inc(hf_made, 1)

            def merge(g, c):
                own = M[:, (g - KEEP) * NJ * IG + c * CH:(g - KEEP) * NJ * IG + (c + 1) * CH].bitcast(U32)
                new = M[:, KEEP * NJ * IG + c * CH:KEEP * NJ * IG + (c + 1) * CH].bitcast(U32)
                pool.wait_ge(mask_made, (g * NCH + c + 1) * 2)
                p.tensor_tensor(own, own, new, ALU.add).then_inc(merged, 1)

            def deviations(g):
                pool.wait_ge(var_made, g + 1)
                p.tensor_scalar(gve[:, :], gmv3[:, :, 1], EPS, 1.0, ALU.add, ALU.mult).then_inc(pool_epi, 1)
                p.tensor_scalar(gnm[:, :], gmv3[:, :, 0], -SC, 0.0, ALU.mult, ALU.add).then_inc(devs_made, 1)
                pool.wait_ge(pool_epi, g + 1)
                p.tensor_tensor(grs[:, :], gve[:, :], half[:, 0:NB], ALU.pow).then_inc(devs_made, 1)

            steps = [0]

            def e_step(ins):
                steps[0] += 1
                ins.then_inc(e_steps, 1)

            def e_args(lo, hi):
                e, d = et[:, NJ + lo:NJ + hi], et[:, 2 * NJ + lo:2 * NJ + hi]
                e_step(p.tensor_scalar(e, s_cols[:, lo:hi], S[:, 0:1], 1.0, ALU.add, ALU.mult))
                pool.wait_ge(e_steps, steps[0])
                e_step(p.tensor_scalar(ve[:, lo:hi], e, 0.2, 0.0, ALU.mult, ALU.add))
                pool.wait_ge(e_steps, steps[0])
                e_step(p.tensor_tensor(d, ve[:, lo:hi], e, ALU.subtract))
                pool.wait_ge(e_steps, steps[0])
                e_step(p.tensor_scalar(e, d, -1.0, 0.0, ALU.mult, ALU.min))
                pool.wait_ge(e_steps, steps[0])
                e_step(p.tensor_scalar(d, d, 1.0, 0.0, ALU.mult, ALU.min))

            def late_scores():
                k = NJ - early
                pool.wait_ge(lone_summed, 1)
                pool.wait_ge(xab_made, 2 * NCH)
                prod = work[:, 0:k * F].rearrange("p (b f) -> p b f", f=F)
                p.tensor_tensor(prod, hc[:, early * F:].rearrange("p (b f) -> p b f", f=F),
                                wa[:, 0:F].unsqueeze(1).to_broadcast([P, k, F]), ALU.mult).then_inc(si_added, 1)
                half_of, n = F // 2, 1
                while half_of >= 1:
                    pool.wait_ge(si_added, n)
                    p.tensor_tensor(prod[:, :, 0:half_of], prod[:, :, 0:half_of], prod[:, :, half_of:2 * half_of],
                                    ALU.add).then_inc(si_added, 1)
                    half_of, n = half_of // 2, n + 1
                pool.wait_ge(si_added, n)
                p.tensor_tensor(s_cols[:, early:NJ], prod[:, :, 0], rs[:, early:], ALU.mult).then_inc(si_late, 1)

            early = NT * NB
            for q in range(XQ):
                x_deviations(q)
            pool.wait_ge(x_devs, XQ)
            p.tensor_scalar(rsc[:, :], rs[:, :], SC, 0.0, ALU.mult, ALU.add).then_inc(rsc_made, 1)
            for c in range(SUMS_EARLY):
                sum_hn(c)
            pool.wait_ge(g_made, 1)
            for m in range(1, HF):
                scaled_f(m)
            for m in range(HF, 2 * NCH):
                if m % 2 == 0 and m // 2 >= SUMS_EARLY:
                    sum_hn(m // 2)
                scaled_f(m)
            pool.wait_ge(less_max, 1)
            pool.wait_ge(si_made, 2)
            e_args(0, early)
            late_scores()
            pool.wait_ge(si_late, 1)
            e_args(early, NJ)
            deviations(0)
            pool.wait_ge(si_squared, 1)
            for q in range(P // 32):
                pool.dma_start(s_dram.rearrange("(j q p) -> q j p", q=P // 32, p=32)[q],
                               si_squares[q * 32:(q + 1) * 32, :]).then_inc(row_sent, 16)
            pool.wait_ge(row_sent, 16 * (P // 32))
            pool.dma_start(s_row[:, NT * IG:], s_dram[NT * IG:].partition_broadcast(P)).then_inc(row_here, 16)
            for g in range(1, KEEP - 1):
                deviations(g)
            pool.wait_ge(neg_made, KEEP * NCH)
            for g in range(KEEP, KEEP + MERGED):
                for c in range(NCH):
                    merge(g, c)
                    if c == NCH // 2 - 1:
                        deviations(g - 1)
            deviations(NG - 2)
            deviations(NG - 1)

        @block.scalar
        def _(act):
            a = nc.scalar.activation
            act.dma_start(a2[:, :], a_in).then_inc(a_here, 16)
            act.dma_start(w0[:, :], w0_in).then_inc(w0_here, 16)
            early = NT * NB
            for q in range(XQ):
                act.wait_ge(nm_made, q + 1)
                for j in range(q * QB, (q + 1) * QB):
                    ins = a(hc[:, j * F:(j + 1) * F], x[:, j * F:(j + 1) * F], ACT.Relu, bias=nm[:, j:j + 1])
                    if j % NB == NB - 1:
                        ins.then_inc(hc_made, 1)
                if q == 0:
                    act.wait_ge(wa_summed, 1)
                    a(wa[:, :], aux[3][:, 0:2 * F + 2], ACT.Copy).then_inc(wa_made, 1)
                    act.wait_ge(ht_turned, 1)
                    a(hT[:, 0:IG], acc[0][:, :], ACT.Copy).then_inc(ht_by_act, 1)
                if q == 2:
                    act.wait_ge(si_turned, 1)
                    a(s_turned[0:NB, :], aux[0][0:NB, 0:P], ACT.Copy).then_inc(s_turned_made, 1)

            def row_for_keys(g):
                act.wait_ge(act_keys, g * NCH)
                a(s_now[:, :], s_row[:, ds(g * IG, IG)], ACT.Copy).then_inc(row_now, 1)

            def keys_free(g, c, t):
                if c == 0:
                    act.wait_ge(row_now, g + 1)
                if not (isinstance(t, int) and t < 2):
                    act.wait_ge(neg_made, t - 1)

            def keys(c, n=KACT):
                o = (c % 2) * CH
                for k in range(n):
                    j = c * CJ + k
                    last = a(key[:, o + k * IG:o + (k + 1) * IG].bitcast(F8), s_now[:, :], ACT.Relu,
                             bias=bsj[:, j:j + 1], scale=BIG, saturate=False)
                last.then_inc(act_keys, 1)

            def mask(g, h, late=False):
                b = h % RAW
                act.wait_ge(raw_here[b], 16 * (g * (2 * NCH // RAW) + h // RAW + 1))
                a(M[:, ds(slot(g, late) + h * HJ * IG, HJ * IG)],
                  raw[:, b * HJ * IG:(b + 1) * HJ * IG],
                  ACT.Copy, scale=float(TWO if late else ONE)).then_inc(mask_made, 1)

            def masks(g, c, late=False):
                for k in range(2):
                    mask(g, 2 * c + k, late)

            def high_part(g, b):
                act.wait_ge(block_summed, g * (NCH * NB) + ((NCH - 1) * NB + b + 1))
                a(u[:, b * W:(b + 1) * W], acc[b][:, 0:W], ACT.Copy,
                  scale=Es[:, ds(g * NB + b, 1)]).then_inc(u_high, 1)

            def turned(g):
                act.wait_ge(u_turned, g + 1)
                a(uT[:, :], aux[2][:, :], ACT.Copy).then_inc(ut_here, 1)

            def centred(g):
                act.wait_ge(devs_made, 2 * g + 2)
                for b in range(NB):
                    last = a(tt[:, b * F:(b + 1) * F], x[:, ds(g * IG + b * F, F)], ACT.Relu,
                             bias=gnm[:, b:b + 1], scale=SC)
                last.then_inc(act_scaled, 1)
                act.wait_ge(act_scaled, g + 1)
                for b in range(NB):
                    last = a(h2[:, ds(g * 2 * IG + 2 * b * F, F)], tt[:, b * F:(b + 1) * F], ACT.Copy,
                             scale=grs[:, b:b + 1])
                last.then_inc(act_high, 1)

            def made_e(lo, hi):
                a(Es[:, :].rearrange("p (k j) -> p k j", k=2)[:, :, lo:hi],
                  et[:, NJ:].rearrange("p (k j) -> p k j", k=2)[:, :, lo:hi], ACT.Exp).then_inc(e_made, 1)

            def high_of_f(m):
                c, k = divmod(m, 2)
                if m == 0:
                    act.wait_ge(hf_first, 1)
                else:
                    act.wait_ge(hf_made, m)
                a((XA, XB)[k][:, c * NB:(c + 1) * NB, 0, 0:F],
                  hf[:, (m % HF) * IG:(m % HF + 1) * IG].rearrange("p (b f) -> p b f", f=F),
                  ACT.Copy).then_inc(xab_high, 1)

            act.wait_ge(row_summed, 1)
            a(s_row[:, 0:IG], aux[0][:, :], ACT.Copy).then_inc(row_made, 1)
            a(s_now[:, :], aux[0][:, :], ACT.Copy).then_inc(row_now, 1)
            masks(0, 0)
            mask(0, 2)
            act.wait_ge(sj_made, 2)
            keys_free(0, 0, 0)
            keys(0)
            act.wait_ge(less_max, 1)
            a(Fs[:, 0:NJ], et[:, 0:NJ], ACT.Exp).then_inc(f_made, 1)
            a(Fs[:, NJ:], et[:, 0:NJ], ACT.Exp, scale=0.2).then_inc(f_made, 1)
            act.wait_ge(f_made, 2)
            for k, X in enumerate((XA, XB)):
                a(X[:, :, 0, F], Fs[:, k * NJ:(k + 1) * NJ], ACT.Copy, scale=SC).then_inc(f_high, 1)
            act.wait_ge(si_turned, 2)
            a(s_turned[:, :], aux[0][0:early, 0:P], ACT.Copy).then_inc(s_turned_made, 1)
            mask(0, 3)
            high_of_f(0)
            high_of_f(1)
            for c in range(NCH - 1):
                high_of_f(2 * c + 2)
                high_of_f(2 * c + 3)
                keys_free(0, c + 1, c + 1)
                keys(c + 1)
                if c + 2 < NCH:
                    masks(0, c + 2)
                if c < NT - 1:
                    act.wait_ge(row_summed, c + 2)
                    a(s_row[:, (c + 1) * IG:(c + 2) * IG], aux[1 - c][:, :], ACT.Copy).then_inc(row_made, 1)
            act.wait_ge(e_steps, 5)
            made_e(0, early)
            act.wait_ge(e_made, 1)

            def slot_free(g, c):
                act.wait_ge(merged, (g - KEEP - 1) * NCH + (c + 1))

            def next_group(g, late=False, reused=False):
                row_for_keys(g)
                if reused:
                    slot_free(g, 0)
                keys_free(g, 0, g * NCH)
                masks(g, 0, late)
                keys(0)

            def group(g, late=False, reused=False):
                if reused:
                    slot_free(g, 1)
                keys_free(g, 1, g * NCH + 1)
                mask(g, 2, late)
                high_part(g - 1, 0)
                mask(g, 3, late)
                high_part(g - 1, 1)
                high_part(g - 1, 2)
                high_part(g - 1, 3)
                keys(1)
                for c in range(2, NCH):
                    if reused:
                        slot_free(g, c)
                    keys_free(g, c, g * NCH + c)
                    masks(g, c, late)
                    keys(c)
                    if c == 4:
                        turned(g - 1)
                    if c == 6:
                        centred(g - 1)

            act.wait_ge(row_made, NT)
            next_group(1)
            group(1)
            act.wait_ge(e_steps, 10)
            made_e(early, NJ)
            act.wait_ge(e_made, 2)
            with act.Fori(2, KEEP) as g:
                next_group(g)
                group(g)
                act.wait_ge(row_here, 16)
            next_group(KEEP, late=True)
            group(KEEP, late=True)
            with act.Fori(KEEP + 1, NG) as g:
                next_group(g, late=True, reused=True)
                group(g, late=True, reused=True)
            for b in range(NB):
                high_part(NG - 1, b)
            turned(NG - 1)
            centred(NG - 1)
            for r, (g, _, nb) in enumerate(ROUNDS):
                act.wait_ge(agg_summed, r + 1)
                if r >= 1:
                    act.wait_ge(y_made, r)
                one = 2.0 if g >= KEEP else 1.0
                a(uT[:, 0:nb * P], aux[r % 4][:, 0:nb * P], ACT.Copy, scale=1.0 / (one * SC)).then_inc(agg_here, 1)

        @block.vector
        def _(dve):
            v = nc.vector
            x1_due = dve.alloc_register("x1_due")
            stats_due = dve.alloc_register("stats_due")
            n = [0]

            def step(ins):
                n[0] += 1
                ins.then_inc(dve_steps, 1)

            def settle():
                dve.wait_ge(dve_steps, n[0])

            def statistics(q):
                for h in (2 * q, 2 * q + 1):
                    dve.wait_ge(x_here[h], 16)
                    for j in range(h * HB, (h + 1) * HB):
                        last = v.bn_stats(st[:, j * 6:(j + 1) * 6], x[:, j * F:(j + 1) * F])
                    last.then_inc(stats_made, 1)
                for h in (2 * q, 2 * q + 1):
                    dve.wait_ge(stats_made, h + 1)
                    for j in range(h * HB, (h + 1) * HB):
                        last = v.bn_aggr(mv[:, 2 * j:2 * j + 2], st[:, j * 6:(j + 1) * 6])
                last.then_inc(x_stats, 1)

            calls = [0]

            def scores(g):
                if calls[0] >= 2:
                    dve.wait_ge(scores_made, calls[0] - 1)
                calls[0] += 1
                dve.wait_ge(hc_made, g + 1)
                for j in range(g * NB, (g + 1) * NB):
                    last = v.tensor_tensor_reduce(
                        out=products[:, j % QB * F:(j % QB + 1) * F], in0=hc[:, j * F:(j + 1) * F],
                        in1=wa[:, F:2 * F], scale=1.0, scalar=0.0, op0=ALU.mult, op1=ALU.add,
                        accum_out=sj_raw[:, j:j + 1])
                last.then_inc(scores_made, 1)

            def turned_x(g):
                dve.wait_ge(ht_turned, g + 1)
                v.tensor_copy(hT[:, g * IG:(g + 1) * IG], acc[g][:, :]).then_inc(ht_by_dve, 1)

            cols = aux[1][:, 0:2 * NT * NB].rearrange("p (j k) -> p j k", k=2)
            sj = s_cols[:, NJ:2 * NJ]
            early = NT * NB
            statistics(0)
            dve.wait_ge(a_here, 16)
            for k in range(2):
                v.tensor_copy(uT[:, k * F:(k + 1) * F], a2[:, k:k + 1].to_broadcast([P, F])).then_inc(a_spread, 1)
            statistics(1)
            statistics(2)
            turned_x(1)
            dve.wait_ge(cols_summed, 1)
            dve.wait_ge(x_devs, 1)
            v.tensor_tensor(s_cols[:, 0:NB], cols[:, 0:NB, 0], rs[:, 0:NB], ALU.mult).then_inc(si_made, 1)
            statistics(3)
            turned_x(2)
            dve.wait_ge(wa_made, 1)
            for g in range(NT, NG):
                scores(g)
            dve.wait_ge(cols_summed, NT)
            dve.wait_ge(x_devs, XQ)
            step(v.tensor_tensor(sj[:, 0:early], cols[:, :, 1], rs[:, 0:early], ALU.mult))
            dve.wait_ge(scores_made, NG - NT)
            step(v.tensor_tensor(sj[:, early:], sj_raw[:, early:], rs[:, early:], ALU.mult))
            settle()
            step(v.reduce_max(smx[:, :], sj, AX_X))
            settle()
            v.tensor_scalar(tt[:, 0:P], ident[:, :], smx[:, 0:1], None, ALU.mult).then_inc(smax_made, 1)
            v.tensor_scalar(bsj[:, :], sj, BIG, None, ALU.mult).then_inc(sj_made, 1)
            v.tensor_scalar(nsj[:, :], sj, -1.0, None, ALU.mult).then_inc(sj_made, 1)
            v.tensor_tensor(s_cols[:, NB:early], cols[:, NB:, 0], rs[:, NB:early], ALU.mult).then_inc(si_made, 1)

            def keys(g, c, t, n=KACT, end=CJ):
                o = (c % 2) * CH
                for k in range(n, end):
                    j = c * CJ + k
                    last = v.tensor_scalar(key[:, o + k * IG:o + (k + 1) * IG], s_row[:, ds(g * IG, IG)],
                                           nsj[:, j:j + 1], float(KEY), ALU.is_gt, ALU.mult)
                if end == CJ:
                    last.then_inc(keys_made, 1)

            def low_of_f(m):
                c, k = divmod(m, 2)
                X = (XA, XB)[k]
                dve.wait_ge(xab_high, m + 1)
                v.tensor_tensor(X[:, c * NB:(c + 1) * NB, 1, 0:F],
                                hf[:, (m % HF) * IG:(m % HF + 1) * IG].rearrange("p (b f) -> p b f", f=F),
                                X[:, c * NB:(c + 1) * NB, 0, 0:F], ALU.subtract).then_inc(xab_made, 1)

            def split_pos(g, c, t, late=False):
                o = (c % 2) * CH
                m = M[:, ds(slot(g, late) + c * CH, CH)].bitcast(U32)
                dve.wait_ge(mask_made, t * 2 + 2)
                dve.wait_ge(act_keys, t + 1)
                if not (isinstance(t, int) and t < 2):
                    dve.wait_ge(block_summed, (t - 1) * NB)
                dve.wait_ge(keys_made, t + 1)
                v.tensor_tensor(pos[:, o:o + CH].bitcast(U32), m, key[:, o:o + CH].bitcast(U32),
                                ALU.bitwise_and).then_inc(pos_made, 1)

            def split_neg(g, c, t, late=False):
                o = (c % 2) * CH
                m = M[:, ds(slot(g, late) + c * CH, CH)].bitcast(U32)
                dve.wait_ge(pos_made, t + 1)
                v.tensor_tensor(neg[:, o:o + CH].bitcast(U32), m, pos[:, o:o + CH].bitcast(U32),
                                ALU.bitwise_xor).then_inc(neg_made, 1)

            def split(g, c, t, late):
                split_pos(g, c, t, late)
                split_neg(g, c, t, late)

            def gather(g, blocks):
                for b in blocks:
                    ub = u[:, b * W:(b + 1) * W]
                    dve.wait_ge(u_high, g * NB + b + 1)
                    v.scalar_tensor_tensor(ub, acc[b][:, W:2 * W], Es[:, ds(g * NB + b, 1)], ub,
                                           ALU.mult, ALU.add).then_inc(u_low, 1)
                for b in blocks:
                    ub = u[:, b * W:(b + 1) * W]
                    dve.wait_ge(u_low, g * NB + b + 1)
                    v.scalar_tensor_tensor(ub, acc[b][:, 2 * W:3 * W], Es[:, ds(g * NB + (NJ + b), 1)], ub,
                                           ALU.mult, ALU.add).then_inc(u_made, 1)

            def complete(g):
                uw = u[:, :].rearrange("p (b w) -> p b w", w=W)
                dve.wait_ge(u_made, g * NB + NB)
                v.tensor_scalar(z[:, :], uw[:, :, F], 0.0, None, ALU.is_equal).then_inc(dve_epi, 1)
                dve.wait_ge(dve_epi, g * EPI + 1)
                for b in range(NB):
                    ub = u[:, b * W:(b + 1) * W]
                    last = v.scalar_tensor_tensor(ub, lone[:, :], z[:, b:b + 1], ub, ALU.mult, ALU.add)
                last.then_inc(u_whole, 1)
                dve.wait_ge(u_whole, g + 1)
                v.reciprocal(rv[:, :], uw[:, :, F]).then_inc(dve_epi, 1)

            def residual(g):
                dve.wait_ge(att_made, g + 1)
                dve.wait_ge(dve_epi, g * EPI + 2)
                for b in range(NB):
                    xb = x[:, ds(g * IG + b * F, F)]
                    last = v.scalar_tensor_tensor(xb, aux[3][:, b * F:(b + 1) * F], rv[:, b:b + 1], xb,
                                                  ALU.mult, ALU.add)
                last.then_inc(x1_made, 1)
                if isinstance(g, int):
                    dve.wait_ge(x1_made, g + 1)
                else:
                    wait_next(dve, x1_made, x1_due, 1)
                for b in range(NB):
                    last = v.bn_stats(gst[:, b * 6:(b + 1) * 6], x[:, ds(g * IG + b * F, F)])
                last.then_inc(dve_epi, 1)
                if isinstance(g, int):
                    dve.wait_ge(dve_epi, g * EPI + 3)
                else:
                    wait_next(dve, dve_epi, stats_due, EPI)
                for b in range(NB):
                    last = v.bn_aggr(gmv[:, 2 * b:2 * b + 2], gst[:, b * 6:(b + 1) * 6])
                last.then_inc(var_made, 1)

            def low_normal(g):
                dve.wait_ge(act_high, g + 1)
                for b in range(NB):
                    last = v.scalar_tensor_tensor(h2[:, ds(g * 2 * IG + (2 * b + 1) * F, F)],
                                                  tt[:, b * F:(b + 1) * F], grs[:, b:b + 1],
                                                  h2[:, ds(g * 2 * IG + 2 * b * F, F)],
                                                  ALU.mult, ALU.subtract)
                last.then_inc(h2_made, 1)

            dve.wait_ge(row_made, 1)
            dve.wait_ge(sj_made, 2)
            keys(0, 0, 0, KACT, KACT + 1)
            dve.wait_ge(smax_spread, 1)
            step(v.reduce_max(S[:, :], aux[2][:, 0:P], AX_X))
            settle()
            v.tensor_scalar(et[:, 0:NJ], sj, S[:, 0:1], None, ALU.subtract).then_inc(less_max, 1)
            keys(0, 0, 0, KACT + 1)
            dve.wait_ge(rsc_made, 1)
            dve.wait_ge(f_made, 2)
            v.tensor_tensor(Gs[:, :].rearrange("p (k j) -> p k j", k=2), Fs[:, :].rearrange("p (k j) -> p k j", k=2),
                            rsc[:, :].unsqueeze(1).to_broadcast([P, 2, NJ]), ALU.mult).then_inc(g_made, 1)
            dve.wait_ge(g_made, 1)
            v.tensor_tensor(hf[:, 0:IG].rearrange("p (b f) -> p b f", f=F),
                            hc[:, 0:IG].rearrange("p (b f) -> p b f", f=F),
                            Gs[:, 0:NB].unsqueeze(2).to_broadcast([P, NB, F]), ALU.mult).then_inc(hf_first, 1)
            split_pos(0, 0, 0)
            dve.wait_ge(f_high, 2)
            for k, X in enumerate((XA, XB)):
                last = v.scalar_tensor_tensor(X[:, :, 1, F], Fs[:, k * NJ:(k + 1) * NJ], SC, X[:, :, 0, F],
                                              ALU.mult, ALU.subtract)
            last.then_inc(f_cols, 1)
            low_of_f(0)
            split_neg(0, 0, 0)
            low_of_f(1)
            for c in range(NCH - 1):
                keys(0, c + 1, c + 1)
                low_of_f(2 * c + 2)
                split_pos(0, c + 1, c + 1)
                low_of_f(2 * c + 3)
                split_neg(0, c + 1, c + 1)
            dve.wait_ge(row_made, NT)
            keys(1, 0, NCH)
            dve.wait_ge(lone_summed, 1)
            v.tensor_copy(lone[:, 0:F], aux[1][:, P:2 * P]).then_inc(lone_made, 1)

            def group(g, late=False):
                t = g * NCH
                keys(g, 1, t + 1)
                split(g, 0, t, late)
                gather(g - 1, [0])
                gather(g - 1, [1])
                gather(g - 1, [2, 3])
                split(g, 1, t + 1, late)
                complete(g - 1)
                for c in range(2, NCH):
                    keys(g, c, t + c)
                    if c == NCH - 1 and not (isinstance(g, int) and g == NG - 1):
                        if not isinstance(g, int):
                            dve.wait_ge(row_here, 16)
                        keys(g + 1, 0, t + NCH)
                    split(g, c, t + c, late)
                    if c == 4:
                        residual(g - 1)
                    if c == 6:
                        low_normal(g - 1)
                    if c == 3 and isinstance(g, int) and g == 1:
                        dve.wait_ge(si_late, 1)
                        v.transpose(si_squares[:, :], s_cols[:, 0:NJ]).then_inc(si_squared, 1)

            def loop_from(g):
                dve.reg_mov(x1_due, g)
                dve.reg_mov(stats_due, g * EPI)

            group(1)
            loop_from(2)
            with dve.Fori(2, KEEP) as g:
                group(g)
            loop_from(KEEP)
            with dve.Fori(KEEP, NG - 1) as g:
                group(g, late=True)
            group(NG - 1, late=True)
            gather(NG - 1, [0])
            gather(NG - 1, [1, 2])
            gather(NG - 1, [3])
            complete(NG - 1)
            residual(NG - 1)
            low_normal(NG - 1)
            dve.wait_ge(block_summed, NG * NCH * NB)
            dve.wait_ge(merged, MERGED * NCH)
            for m in range(MERGED):
                own = M[:, m * NJ * IG:(m + 1) * NJ * IG].bitcast(U32)
                v.tensor_scalar(apart_of(m).bitcast(U32), own, TWO * 0x01010101, None,
                                ALU.bitwise_and).then_inc(apart, 1)
                dve.wait_ge(apart, 2 * m + 1)
                v.tensor_scalar(own, own, ONE * 0x01010101, None, ALU.bitwise_and).then_inc(apart, 1)
            dve.wait_ge(w_here, 48)
            for r, (g, b0, nb) in enumerate(ROUNDS):
                before = blocks_before(r)
                dve.wait_ge(y_made, r + 1)
                if r >= 1:
                    dve.wait_ge(o_made, before)
                for b in range(nb):
                    v.tensor_tensor(tt[:, b * F:(b + 1) * F], acc[r % 2][:, b * F:(b + 1) * F], b1[:, :],
                                    ALU.add).then_inc(y_used, 1)
                for b in range(nb):
                    dve.wait_ge(y_used, before + b + 1)
                    xb = x[:, g * IG + (b0 + b) * F:g * IG + (b0 + b + 1) * F]
                    v.scalar_tensor_tensor(xb, tt[:, b * F:(b + 1) * F], 0.0, xb, ALU.max,
                                           ALU.add).then_inc(o_made, 1)

        @block.tensor
        def _(pe):
            mm = nc.tensor.matmul
            chunks_due = pe.alloc_register("chunks_due")
            pe.reg_mov(chunks_due, NCH + 1)
            banks_due = pe.alloc_register("banks_due")
            pe.reg_mov(banks_due, 1)
            def warm(n):
                for _ in range(n):
                    mm(aux[3][:, P:2 * P], ones[:, :], ones[:, :], start=True, stop=True, skip_group_check=True)

            pe.wait_ge(a_spread, 2)
            pe.wait_ge(w0_here, 16)
            for k in range(2):
                last = mm(aux[3][:, k * F:(k + 1) * F], uT[:, k * F:(k + 1) * F], w0[:, :], start=True, stop=True,
                          skip_group_check=True)
            mm(aux[3][:, 2 * F:2 * F + 2], w0[:, :], a2[:, :], start=True, stop=True,
               skip_group_check=True).then_inc(wa_summed, 1)

            def turn_x(g):
                pe.wait_ge(hc_made, g + 1)
                for b in range(NB):
                    j = g * NB + b
                    last = nc.tensor.transpose(acc[g][:, b * P:(b + 1) * P], hc[:, j * F:(j + 1) * F], ident[:, :])
                last.then_inc(ht_turned, 1)

            def cols(g):
                for b in range(NB):
                    j = g * NB + b
                    last = mm(aux[1][:, 2 * j:2 * j + 2], hT[:, j * P:(j + 1) * P], wa[:, 2 * F:2 * F + 2],
                              start=True, stop=True, skip_group_check=True)
                last.then_inc(cols_summed, 1)

            def row(g):
                for b in range(NB):
                    j, k = g * NB + b, NB if g == 0 else NT * NB
                    last = mm(aux[g % 2][:, b * P:(b + 1) * P], ident[0:k, j:j + 1].to_broadcast([k, P]),
                              s_turned[0:k, :], start=True, stop=True, skip_group_check=True)
                last.then_inc(row_summed, 1)

            pe.wait_ge(ident_made, 1)
            turn_x(0)
            turn_x(1)
            pe.wait_ge(wa_made, 1)
            pe.wait_ge(ht_by_act, 1)
            cols(0)
            turn_x(2)
            pe.wait_ge(si_made, 1)
            nc.tensor.transpose(aux[0][0:NB, 0:P], s_cols[:, 0:NB], ident[:, :]).then_inc(si_turned, 1)
            pe.wait_ge(ht_by_dve, 1)
            cols(1)
            pe.wait_ge(s_turned_made, 1)
            row(0)
            pe.wait_ge(ht_by_dve, 2)
            cols(2)
            warm(WARM)
            pe.wait_ge(smax_made, 1)
            mm(aux[2][:, 0:P], ones[:, :], tt[:, 0:P], start=True, stop=True,
               skip_group_check=True).then_inc(smax_spread, 1)
            pe.wait_ge(si_made, 2)
            pe.wait_ge(row_now, 1)
            nc.tensor.transpose(aux[0][0:NT * NB, 0:P], s_cols[:, 0:NT * NB], ident[:, :]).then_inc(si_turned, 1)
            warm(WARM + 2)
            pe.wait_ge(s_turned_made, 2)
            row(1)
            warm(WARM)

            def chunk(g, c, t):
                o = (c % 2) * CH
                if isinstance(t, int):
                    pe.wait_ge(neg_made, t + 1)
                else:
                    wait_next(pe, neg_made, chunks_due, 1)
                if isinstance(t, int):
                    pe.wait_ge(xab_made, 2 * c + 2)
                for b in range(NB):
                    if c == 0:
                        if not isinstance(t, int):
                            wait_next(pe, u_made, banks_due, 1)
                    for k in range(CJ):
                        j = c * CJ + k
                        first, end = j == 0, j == NJ - 1
                        q = o + k * IG + b * P
                        dp = pos[:, q:q + P].bitcast(F8)
                        dn = neg[:, q:q + P].bitcast(F8)
                        mm(acc[b][:, 0:2 * W], dp, XA[:, j, :, :].rearrange("p k w -> p (k w)"),
                           start=first, stop=end, skip_group_check=True)
                        mm(acc[b][:, 2 * W:3 * W], dn, XB[:, j, 0, :], start=False, stop=False,
                           skip_group_check=True)
                        last = mm(acc[b][:, 2 * W:3 * W], dn, XB[:, j, 1, :], start=False, stop=end,
                                  skip_group_check=True)
                    last.then_inc(block_summed, 1)

            def first_chunk():
                pe.wait_ge(f_cols, 1)
                pe.wait_ge(pos_made, 1)
                pe.wait_ge(xab_made, 1)
                for b in range(NB):
                    for j in range(CJ):
                        q = j * IG + b * P
                        mm(acc[b][:, 0:2 * W], pos[:, q:q + P].bitcast(F8),
                           XA[:, j, :, :].rearrange("p k w -> p (k w)"), start=(j == 0), stop=False,
                           skip_group_check=True)
                pe.wait_ge(neg_made, 1)
                pe.wait_ge(xab_made, 2)
                for b in range(NB):
                    for j in range(CJ):
                        q = j * IG + b * P
                        for k in range(2):
                            last = mm(acc[b][:, 2 * W:3 * W], neg[:, q:q + P].bitcast(F8), XB[:, j, k, :],
                                      start=False, stop=False, skip_group_check=True)
                    last.then_inc(block_summed, 1)

            def turn(g):
                pe.wait_ge(u_whole, g + 1)
                for b in range(NB):
                    last = nc.tensor.transpose(aux[2][:, b * P:(b + 1) * P], u[:, b * W:b * W + F], ident[:, :])
                last.then_inc(u_turned, 1)

            def project(g):
                pe.wait_ge(ut_here, g + 1)
                for b in range(NB):
                    last = mm(aux[3][:, b * F:(b + 1) * F], uT[:, b * P:(b + 1) * P], w0t[:, :],
                              start=True, stop=True, skip_group_check=True)
                last.then_inc(att_made, 1)

            first_chunk()
            row(2)
            for c in range(1, NCH):
                chunk(0, c, c)
                if c == 6:
                    pe.wait_ge(hsum_made, NG)
                    pe.wait_ge(row_made, 2)
                    for b in range(NB):
                        last = mm(aux[1][:, P:2 * P], ones[:, :], hsum[:, b * F:(b + 1) * F], start=(b == 0),
                                  stop=(b == NB - 1), skip_group_check=True)
                    last.then_inc(lone_summed, 1)
            pe.wait_ge(w_here, 48)
            with pe.Fori(1, NG) as g:
                for c in range(NCH):
                    chunk(g, c, g * NCH + c)
                    if c == 1:
                        turn(g - 1)
                    if c == 2:
                        project(g - 1)

            def project_y(r):
                pe.wait_ge(agg_here, r + 1)
                if r >= 2:
                    pe.wait_ge(o_made, blocks_before(r - 1))
                for b in range(ROUNDS[r][2]):
                    last = mm(acc[r % 2][:, b * F:(b + 1) * F], uT[:, b * P:(b + 1) * P], w1[:, :],
                              start=True, stop=True, skip_group_check=True)
                last.then_inc(y_made, 1)

            def aggregate(r, j):
                g, b0, nb = ROUNDS[r]
                if KEEP <= g < NG - 1:
                    src = apart_of(g - KEEP)
                else:
                    src = M[:, slot(g, g >= KEEP):slot(g, g >= KEEP) + NJ * IG]
                if j == 0 and r >= 2:
                    pe.wait_ge(apart, min(r, NG - 1) - 1)
                if j == 0 and r >= 4:
                    pe.wait_ge(agg_here, r - 3)
                for k in range(2):
                    last = mm(aux[r % 4][:, 0:nb * P], h2[:, (2 * j + k) * F:(2 * j + k + 1) * F],
                              src[:, j * IG + b0 * P:j * IG + (b0 + nb) * P].bitcast(F8),
                              start=(j == 0 and k == 0), stop=(j == NJ - 1 and k == 1))
                if j == NJ - 1:
                    last.then_inc(agg_summed, 1)

            for r in range(2):
                for j in range(NJ - NB):
                    if r == 0 and j % NB == 0:
                        pe.wait_ge(h2_made, j // NB + 1)
                    aggregate(r, j)
                    if r == 0 and j == 7:
                        turn(NG - 1)
                    if r == 0 and j == 15:
                        project(NG - 1)
            pe.wait_ge(h2_made, NG)
            for r in range(2):
                for j in range(NJ - NB, NJ):
                    aggregate(r, j)
            for r in range(2, len(ROUNDS)):
                for j in range(NJ):
                    aggregate(r, j)
                    if j == 11:
                        project_y(r - 1 if r > 2 else 0)
                    if r == 2 and j == 19:
                        project_y(1)
            project_y(len(ROUNDS) - 1)


def kernel(x, adj, L0_gnn_W, L0_gnn_a, L1_gnn_W, L1_gnn_b):
    import numpy as np
    import concourse.bacc as bacc
    from concourse.bass_utils import run_bass_kernel_spmd

    def flat(a):
        return np.ascontiguousarray(a)

    x, adj, w0, a, w1, b1 = (np.asarray(t) for t in (x, adj, L0_gnn_W, L0_gnn_a, L1_gnn_W, L1_gnn_b))
    arrays = {
        "x_dram": flat(x.reshape(NJ, P, F).transpose(1, 0, 2)).reshape(P, NJ * F),
        "adj_dram": flat(adj.T.reshape(NJ, P, NG, IG).transpose(2, 1, 0, 3)).reshape(NG * P, NJ * IG),
        "w0_dram": flat(w0),
        "w0t_dram": flat(w0.T),
        "a_dram": flat(a.reshape(2, F).T),
        "w1_dram": flat(w1),
        "b1_dram": flat(b1),
    }
    nc = bacc.Bacc("TRN2", target_bir_lowering=False, num_devices=1)
    args = [nc.dram_tensor(k, t.shape, mybir.dt.from_np(t.dtype), kind="ExternalInput").ap()
            for k, t in arrays.items()]
    out = nc.dram_tensor("out_dram", (P, NJ * F), F32, kind="ExternalOutput").ap()
    s_dram = nc.dram_tensor("s_dram", (N,), F32, kind="Internal").ap()
    gat_sum_kernel(nc, *args, out, s_dram)
    r = run_bass_kernel_spmd(nc, [arrays], core_ids=[0])
    got = r.results[0]["out_dram"]
    return flat(got.reshape(P, NJ, F).transpose(1, 0, 2)).reshape(N, F)
```
